# Optimizing a Trainium2 kernel written in Bass

```python
import numpy as np
import jax
import jax.numpy as jnp

def _softmax(x, axis=-1):
    return jax.nn.softmax(x, axis=axis)

def _gelu(x):
    return jax.nn.gelu(x, approximate=True)

def _silu(x):
    return jax.nn.silu(x)

def _sigmoid(x):
    return jax.nn.sigmoid(x)

def _layernorm(x, axis=-1, eps=1e-05):
    m = jnp.mean(x, axis=axis, keepdims=True)
    v = jnp.var(x, axis=axis, keepdims=True)
    return (x - m) / jnp.sqrt(v + eps)

def _scatter_add(tgt, idx, src, axis=0):
    return tgt.at[idx].add(src)

def _segment_sum(src, seg, n):
    return jax.ops.segment_sum(src, seg, n)
kernel_name = 'mk_cond_seq_d2_seqx_r2_c563f6'

def setup_inputs(seed: int=0):
    np.random.seed(seed)
    _w = jnp.asarray

    def _rec_inputs():
        import jax
        import jax.numpy as jnp
        _rk = jax.random.key(seed)
        x = 7.22e-05 + 1 * jax.random.normal(jax.random.fold_in(_rk, 1), (8, 512, 512), jnp.float32)
        _lenS = 512 - jax.random.randint(jax.random.fold_in(_rk, 7), (8,), 0, max(1, 512 // 4) + 1, jnp.int32)
        _lenS2 = 512 - jax.random.randint(jax.random.fold_in(_rk, 8), (8,), 0, max(1, 512 // 4) + 1, jnp.int32)
        cond_2048 = 0.00782532 + 1.00527 * jax.random.normal(jax.random.fold_in(_rk, 11), (8, 1024), jnp.float32)
        _validS = jnp.arange(512)[None, :] < _lenS[:, None]
        _validS2 = jnp.arange(512)[None, :] < _lenS2[:, None]
        _causal = jnp.tril(jnp.ones((512, 512), dtype=bool))
        mask_BxSx1_fk1 = jnp.where(jnp.ones((8, 512, 1), dtype=bool), 1.0, 0.0).astype(jnp.float32)
        mask_BxS_ff1 = jnp.where(jnp.ones((8, 512), dtype=bool), 1.0, 0.0).astype(jnp.float32)
        return (x, cond_2048, mask_BxSx1_fk1, mask_BxS_ff1)
    x, cond_2048, mask_BxSx1_fk1, mask_BxS_ff1 = _rec_inputs()

    def _L0_cond_setup():
        import jax, jax.numpy as jnp
        import numpy as np
        B, T, D, H, TE = (4, 1024, 512, 8, 1024)
        EPS = 1e-05

        def _ln(x, w, b):
            m = jnp.mean(x, axis=-1, keepdims=True)
            v = jnp.mean((x - m) ** 2, axis=-1, keepdims=True)
            return (x - m) * jax.lax.rsqrt(v + EPS) * w + b
        key = jax.random.key(seed)
        ks = jax.random.split(key, 16)
        s = 0.02
        inp = {'x': jax.random.normal(ks[0], (B, T, D), jnp.float32), 'emb': jax.random.normal(ks[1], (B, TE), jnp.float32), 'src_mask': (jax.random.uniform(ks[2], (B, T, 1)) > 0.2).astype(jnp.float32), 'num_head': H, 'ln_w': jnp.ones((D,), jnp.float32), 'ln_b': jnp.zeros((D,), jnp.float32), 'Wq': jax.random.normal(ks[3], (D, D), jnp.float32) * s, 'bq': jnp.zeros((D,), jnp.float32), 'Wk': jax.random.normal(ks[4], (D, D), jnp.float32) * s, 'bk': jnp.zeros((D,), jnp.float32), 'Wv': jax.random.normal(ks[5], (D, D), jnp.float32) * s, 'bv': jnp.zeros((D,), jnp.float32), 'W_emb': jax.random.normal(ks[6], (TE, 2 * D), jnp.float32) * s, 'b_emb': jnp.zeros((2 * D,), jnp.float32), 'ln2_w': jnp.ones((D,), jnp.float32), 'ln2_b': jnp.zeros((D,), jnp.float32), 'W_out': jax.random.normal(ks[7], (D, D), jnp.float32) * s, 'b_out': jnp.zeros((D,), jnp.float32)}
        return inp
    _L0_cond_all = _L0_cond_setup()
    _L0_cond_in = {k: v for k, v in _L0_cond_all.items() if k in ('ln_w', 'ln_b', 'Wq', 'bq', 'Wk', 'bk', 'Wv', 'bv', 'W_emb', 'b_emb', 'ln2_w', 'ln2_b', 'W_out', 'b_out')}
    del _L0_cond_all

    def _L1_cond_setup():
        import jax, jax.numpy as jnp
        import numpy as np
        B, T, D, H, TE = (8, 512, 512, 16, 1024)
        LN_EPS = 1e-05

        def layer_norm(x, w, b):
            m = jnp.mean(x, axis=-1, keepdims=True)
            v = jnp.var(x, axis=-1, keepdims=True)
            return (x - m) / jnp.sqrt(v + LN_EPS) * w + b
        key = jax.random.key(seed)
        ks = jax.random.split(key, 8)
        s = lambda k, sh: jax.random.normal(k, sh, jnp.float32) * 0.02
        return dict(x=jax.random.normal(ks[0], (B, T, D), jnp.float32), emb=jax.random.normal(ks[1], (B, TE), jnp.float32), src_mask=jnp.ones((B, T), jnp.float32), norm_w=jnp.ones((D,), jnp.float32), norm_b=jnp.zeros((D,), jnp.float32), q_w=s(ks[2], (D, D)), q_b=jnp.zeros((D,), jnp.float32), k_w=s(ks[3], (D, D)), k_b=jnp.zeros((D,), jnp.float32), v_w=s(ks[4], (D, D)), v_b=jnp.zeros((D,), jnp.float32), emb_w=s(ks[5], (TE, 2 * D)), emb_b=jnp.zeros((2 * D,), jnp.float32), sb_norm_w=jnp.ones((D,), jnp.float32), sb_norm_b=jnp.zeros((D,), jnp.float32), out_w=s(ks[6], (D, D)), out_b=jnp.zeros((D,), jnp.float32))
    _L1_cond_all = _L1_cond_setup()
    _L1_cond_in = {k: v for k, v in _L1_cond_all.items() if k in ('norm_w', 'norm_b', 'q_w', 'q_b', 'k_w', 'k_b', 'v_w', 'v_b', 'emb_w', 'emb_b', 'sb_norm_w', 'sb_norm_b', 'out_w', 'out_b')}
    del _L1_cond_all
    return {'x': x, 'cond_2048': cond_2048, 'mask_BxSx1_fk1': mask_BxSx1_fk1, 'mask_BxS_ff1': mask_BxS_ff1, 'L0_cond_ln_w': _L0_cond_in['ln_w'], 'L0_cond_ln_b': _L0_cond_in['ln_b'], 'L0_cond_Wq': _L0_cond_in['Wq'], 'L0_cond_bq': _L0_cond_in['bq'], 'L0_cond_Wk': _L0_cond_in['Wk'], 'L0_cond_bk': _L0_cond_in['bk'], 'L0_cond_Wv': _L0_cond_in['Wv'], 'L0_cond_bv': _L0_cond_in['bv'], 'L0_cond_W_emb': _L0_cond_in['W_emb'], 'L0_cond_b_emb': _L0_cond_in['b_emb'], 'L0_cond_ln2_w': _L0_cond_in['ln2_w'], 'L0_cond_ln2_b': _L0_cond_in['ln2_b'], 'L0_cond_W_out': _L0_cond_in['W_out'], 'L0_cond_b_out': _L0_cond_in['b_out'], 'L1_cond_norm_w': _L1_cond_in['norm_w'], 'L1_cond_norm_b': _L1_cond_in['norm_b'], 'L1_cond_q_w': _L1_cond_in['q_w'], 'L1_cond_q_b': _L1_cond_in['q_b'], 'L1_cond_k_w': _L1_cond_in['k_w'], 'L1_cond_k_b': _L1_cond_in['k_b'], 'L1_cond_v_w': _L1_cond_in['v_w'], 'L1_cond_v_b': _L1_cond_in['v_b'], 'L1_cond_emb_w': _L1_cond_in['emb_w'], 'L1_cond_emb_b': _L1_cond_in['emb_b'], 'L1_cond_sb_norm_w': _L1_cond_in['sb_norm_w'], 'L1_cond_sb_norm_b': _L1_cond_in['sb_norm_b'], 'L1_cond_out_w': _L1_cond_in['out_w'], 'L1_cond_out_b': _L1_cond_in['out_b']}

def reference(x, cond_2048, mask_BxSx1_fk1, mask_BxS_ff1, L0_cond_ln_w, L0_cond_ln_b, L0_cond_Wq, L0_cond_bq, L0_cond_Wk, L0_cond_bk, L0_cond_Wv, L0_cond_bv, L0_cond_W_emb, L0_cond_b_emb, L0_cond_ln2_w, L0_cond_ln2_b, L0_cond_W_out, L0_cond_b_out, L1_cond_norm_w, L1_cond_norm_b, L1_cond_q_w, L1_cond_q_b, L1_cond_k_w, L1_cond_k_b, L1_cond_v_w, L1_cond_v_b, L1_cond_emb_w, L1_cond_emb_b, L1_cond_sb_norm_w, L1_cond_sb_norm_b, L1_cond_out_w, L1_cond_out_b):
    import jax
    import jax.numpy as jnp

    def _L0_cond_ref(x, emb, src_mask, num_head, ln_w, ln_b, Wq, bq, Wk, bk, Wv, bv, W_emb, b_emb, ln2_w, ln2_b, W_out, b_out):
        import jax, jax.numpy as jnp
        import numpy as np
        B, T, D, H, TE = (4, 1024, 512, 8, 1024)
        EPS = 1e-05

        def _ln(x, w, b):
            m = jnp.mean(x, axis=-1, keepdims=True)
            v = jnp.mean((x - m) ** 2, axis=-1, keepdims=True)
            return (x - m) * jax.lax.rsqrt(v + EPS) * w + b
        b, t, d = x.shape
        h = num_head
        dh = d // h
        xn = _ln(x, ln_w, ln_b)
        q = xn @ Wq + bq
        k = xn @ Wk + bk + (1.0 - src_mask) * -1000000.0
        q = jax.nn.softmax(q.reshape(b, t, h, dh), axis=-1)
        k = jax.nn.softmax(k.reshape(b, t, h, dh), axis=1)
        v = ((xn @ Wv + bv) * src_mask).reshape(b, t, h, dh)
        att = jnp.einsum('bnhd,bnhl->bhdl', k, v)
        y = jnp.einsum('bnhd,bhdl->bnhl', q, att).reshape(b, t, d)
        emb_out = (jax.nn.silu(emb) @ W_emb + b_emb)[:, None, :]
        scale, shift = jnp.split(emb_out, 2, axis=2)
        hh = _ln(y, ln2_w, ln2_b) * (1.0 + scale) + shift
        hh = jax.nn.silu(hh) @ W_out + b_out
        return x + hh

    def _L1_cond_ref(x, emb, src_mask, norm_w, norm_b, q_w, q_b, k_w, k_b, v_w, v_b, emb_w, emb_b, sb_norm_w, sb_norm_b, out_w, out_b):
        import jax, jax.numpy as jnp
        import numpy as np
        B, T, D, H, TE = (8, 512, 512, 16, 1024)
        LN_EPS = 1e-05

        def layer_norm(x, w, b):
            m = jnp.mean(x, axis=-1, keepdims=True)
            v = jnp.var(x, axis=-1, keepdims=True)
            return (x - m) / jnp.sqrt(v + LN_EPS) * w + b
        Bx, Tx, Dx = x.shape
        xn = layer_norm(x, norm_w, norm_b)
        q = (xn @ q_w + q_b).reshape(Bx, Tx, H, -1)
        k = (xn @ k_w + k_b).reshape(Bx, Tx, H, -1)
        att = jnp.einsum('bnhl,bmhl->bnmh', q, k)
        mask = src_mask.reshape(Bx, 1, Tx, 1)
        att = att + (1.0 - mask) * -1000000.0
        att = jax.nn.softmax(att, axis=2)
        v = ((xn @ v_w + v_b) * src_mask[:, :, None]).reshape(Bx, Tx, H, -1)
        y = jnp.einsum('bnmh,bmhl->bnhl', att, v).reshape(Bx, Tx, Dx)
        e = jax.nn.silu(emb) @ emb_w + emb_b
        scale, shift = jnp.split(e[:, None, :], 2, axis=2)
        h = layer_norm(y, sb_norm_w, sb_norm_b) * (1.0 + scale) + shift
        h = jax.nn.silu(h) @ out_w + out_b
        return x + h
    x = _L0_cond_ref(x, cond_2048, mask_BxSx1_fk1, 8, L0_cond_ln_w, L0_cond_ln_b, L0_cond_Wq, L0_cond_bq, L0_cond_Wk, L0_cond_bk, L0_cond_Wv, L0_cond_bv, L0_cond_W_emb, L0_cond_b_emb, L0_cond_ln2_w, L0_cond_ln2_b, L0_cond_W_out, L0_cond_b_out)
    x = _L1_cond_ref(x, cond_2048, mask_BxS_ff1, L1_cond_norm_w, L1_cond_norm_b, L1_cond_q_w, L1_cond_q_b, L1_cond_k_w, L1_cond_k_b, L1_cond_v_w, L1_cond_v_b, L1_cond_emb_w, L1_cond_emb_b, L1_cond_sb_norm_w, L1_cond_sb_norm_b, L1_cond_out_w, L1_cond_out_b)
    return x

_drawn_inputs = setup_inputs


def setup_inputs(seed=0):
    import zlib

    import numpy as np

    out = dict(_drawn_inputs(seed))
    spreads = {'L0_cond_ln_w': (1.0, 0.2),
     'L0_cond_ln_b': (0.0, 0.275),
     'L0_cond_bq': (0.0, 0.8),
     'L0_cond_bk': (0.0, 0.1),
     'L0_cond_bv': (0.0, 0.1),
     'L0_cond_b_emb': (0.0, 0.1),
     'L0_cond_ln2_w': (1.0, 0.2),
     'L0_cond_ln2_b': (0.0, 0.289),
     'L0_cond_b_out': (0.0, 0.1),
     'L1_cond_norm_w': (1.0, 0.2),
     'L1_cond_norm_b': (0.0, 0.272),
     'L1_cond_q_b': (0.0, 0.1),
     'L1_cond_k_b': (0.0, 0.1),
     'L1_cond_v_b': (0.0, 0.1),
     'L1_cond_emb_b': (0.0, 0.1),
     'L1_cond_sb_norm_w': (1.0, 0.2),
     'L1_cond_sb_norm_b': (0.0, 0.1),
     'L1_cond_out_b': (0.0, 0.1)}
    factors = {'L0_cond_Wq': 8.0}
    for name, (base, spread) in spreads.items():
        noise = np.random.default_rng([zlib.crc32(name.encode()), seed]).standard_normal(out[name].shape)
        drawn = base * np.exp(spread * noise) if base else spread * noise
        out[name] = jnp.asarray(drawn.astype(out[name].dtype))
    for name, factor in factors.items():
        out[name] = (out[name] * factor).astype(out[name].dtype)
    return out
```

```python
from contextlib import ExitStack

import concourse.bass as bass
from concourse import mybir

ALU = mybir.AluOpType
ACT = mybir.ActivationFunctionType
AX = mybir.AxisListType
F32 = mybir.dt.float32
FR = mybir.dt.float32r

B, T, D, TE = 8, 512, 512, 1024
NT = T // 128
NC = D // 128
EPS = 1e-5
NEG = 1000000.0
H0, H1 = 8, 16
NG = 4
RM, RX, RE = 96, 98, 100



class Counter:

    def __init__(self, handle):
        self.h, self.n = handle, 0

    def add(self, k):
        self.n += k
        return (self, self.n)


class Queues:

    def __init__(self, nc, ctx):
        self.nc, self.ctx, self.sems = nc, ctx, {}
        self.q = {e: [] for e in ("pe", "act", "dve", "pool", "sp")}
        self.seen = {e: {} for e in self.q}

    def sem(self, name):
        if name not in self.sems:
            self.sems[name] = Counter(self.ctx.enter_context(self.nc.semaphore("s_" + name)))
        return self.sems[name]

    def put(self, eng, fn, waits=(), sig=None):
        need = []
        for w in flat(waits):
            if self.seen[eng].get(w[0], 0) < w[1]:
                self.seen[eng][w[0]] = w[1]
                need.append(w)
        s = self.sem(sig) if sig else None
        step = 16 if eng == "sp" else 1
        self.q[eng].append((fn, need, s, step))
        return s.add(step) if s else None

    def run(self, eng, e):
        for fn, need, s, step in self.q[eng]:
            for c, v in need:
                e.wait_ge(c.h, v)
            ins = fn(e)
            if s:
                ins.then_inc(s.h, step)


def flat(ws):
    for w in ws:
        if w is None:
            continue
        if isinstance(w, tuple):
            yield w
        else:
            yield from flat(w)


def raw32(ap):
    return ap.bitcast(F32) if ap.dtype == FR else ap


class Ring:

    def __init__(self, bufs):
        self.bufs = bufs
        self.free = [(i, []) for i in range(len(bufs))]

    def take(self):
        assert self.free, "taken again before its readers were queued"
        i, w = self.free.pop(0)
        return i, self.bufs[i], w

    def release(self, i, *ticks):
        self.free.append((i, list(ticks)))


def interleave(*gens):
    live = [[g, float(w), 0.0] for g, w in gens if g is not None]
    while live:
        it = min(live, key=lambda x: x[2])
        try:
            next(it[0])
            it[2] += 1.0 / it[1]
        except StopIteration:
            live.remove(it)


def part(gen, n):
    for _ in range(n if gen is not None else 0):
        if next(gen, StopIteration) is StopIteration:
            return
        yield


def chain(*gens):
    for g in gens:
        if g is not None:
            yield from g


def cond_two_layers(nc, A, out):
    ctx = ExitStack()
    with ctx:
        Q = Queues(nc, ctx)
        put = Q.put

        def sb(name, shape, dt=F32, c=ctx):
            return c.enter_context(nc.sbuf_tensor(name, shape, dt))

        md = nc.dram_tensor("mask_scratch", [2, B, T], F32, kind="Internal").ap()
        x1d = nc.dram_tensor("x1_scratch", [B, T, D], F32, kind="Internal").ap()

        Wh = {n: sb("Wh_" + n, [128, NC, D], FR) for n in "qkvo"}
        Wl = {n: sb("Wl_" + n, [128, NC, D], FR) for n in "qkvo"}
        xin = sb("xin", [128, NT, D])
        xTh = sb("xTh", [128, NC, T], FR)
        xTl = sb("xTl", [128, NC, T], FR)
        yb = sb("yb", [128, NT, D])
        sTh = sb("sTh", [128, NC, T], FR)
        sTl = sb("sTl", [128, NC, T], FR)
        tb = sb("tb", [128, D])
        ub = sb("ub", [128, D])
        lnb_b = ub[:].rearrange("p (c n) -> p c n", c=NC)
        vt = Ring([sb("vt0", [128, D]), sb("vt1", [128, D])])
        wr = Ring([sb("wr0", [128, D]), sb("wr1", [128, D])])
        bvB = sb("bvB", [128, D])
        boB = sb("boB", [128, D])
        ident = sb("ident", [128, 128])
        ones = sb("ones", [128, 32])
        mhalf = sb("mhalf", [128, NT])
        cols = sb("cols", [128, 24])
        bqc = sb("bqc", [128, NC])
        bkc = sb("bkc", [128, NC])
        mk = sb("mk", [128, B, NT])
        mod = sb("mod", [128, 2, NC, B])
        cT = sb("cT", [128, 8, B])
        cS = sb("cS", [128, 8, B])
        cU = sb("cU", [128, 8, B])
        st = sb("st", [128, 2, NT, 6])
        mv = sb("mv", [128, 2, NT, 2])
        ve = sb("ve", [128, 2, NT])
        rs = sb("rs", [128, 2, NT])
        nm = sb("nm", [128, 2, NT])

        c0 = ExitStack()
        mB = Ring([sb("mB0", [128, T], c=c0)])
        ET = sb("ET", [128, NC, T], c=c0)
        Eh = sb("Eh", [128, NT, D], FR, c=c0)
        El = sb("El", [128, NT, D], FR, c=c0)
        vh = sb("vh", [128, NT, D], FR, c=c0)
        vl = sb("vl", [128, NT, D], FR, c=c0)
        eq = sb("eq", [128, NT, D], c=c0)
        qh = Ring([sb("qh0", [128, T], FR, c=c0), sb("qh1", [128, T], FR, c=c0)])
        ql = Ring([sb("ql0", [128, T], FR, c=c0), sb("ql1", [128, T], FR, c=c0)])
        bqB = sb("bqB", [128, D], c=c0)
        Af = sb("Af", [128, NC, 64], c=c0)
        Ah = sb("Ah", [128, NC, 130], FR, c=c0)
        Al = sb("Al", [128, NC, 130], FR, c=c0)
        qmx = sb("qmx", [128, 2, H0], c=c0)
        kmx = sb("kmx", [128, 2, NC], c=c0)
        kmb = sb("kmb", [128, 2, NC], c=c0)
        knb = sb("knb", [128, 2, NC], c=c0)
        ksm = sb("ksm", [128, 2, NC], c=c0)
        krc = sb("krc", [128, 2, NC], c=c0)
        yrc = sb("yrc", [128, 4], c=c0)
        c0.close()

        c1 = ctx
        Qs = [sb(f"Qs{i}", [128, 4, T], FR, c=c1) for i in range(2)]
        Ks = [sb(f"Ks{i}", [128, 4, T], FR, c=c1) for i in range(2)]
        sg = {n: sb("sg_" + n, [128, T], FR, c=c1) for n in ("qh", "ql", "kh", "kl")}
        vf = sb("vf", [128, NT, D], c=c1)
        Pb = Ring([sb(f"Pb{i}", [128, 4, T], c=c1) for i in range(3)])
        yT = sb("yT", [128, T], c=c1)
        dT = sb("dT", [128, T], c=c1)
        rd = sb("rd", [128, NT, 4], c=c1)
        nx = sb("nx", [128, 2, 16], c=c1)
        nxh = sb("nxh", [16, 128], FR, c=c1)
        nxl = sb("nxl", [16, 128], FR, c=c1)

        ps = [ctx.enter_context(nc.psum_tensor(f"ps{i}", [128, 512], F32)) for i in range(8)]
        work = Ring([ps[0], ps[1]])
        aux = Ring([ps[2], ps[3], ps[4]])
        aux2 = Ring([ps[5], ps[6], ps[7]])
        sbank = Ring([ps[2], ps[3]])
        tbank = Ring([ps[4], ps[5]])

        t_c = put("pool", lambda e: e.memset(ones[:], 1.0), sig="ones")
        t_c0 = put("pool", lambda e: e.memset(ident[:], 0.0), sig="const")
        t_id = put("pool", lambda e: e.affine_select(out=ident[:], in_=ident[:], compare_op=ALU.not_equal,
                                                     fill=1.0, base=0, pattern=[[-1, 128]],
                                                     channel_multiplier=1), [t_c0], sig="const")
        t_mh = put("pool", lambda e: e.memset(mhalf[:], -0.5), sig="const")

        def load(name, dst, src, waits=()):
            return put("sp", lambda e: e.dma_start(raw32(dst), raw32(src)), waits, sig=name)

        t_mk = load("l_mk", mk[:], A["mk"])
        t_cT = load("l_cT", cT[:], A["cT"])

        t = put("act", lambda e: e.activation(cS[:], cT[:], ACT.Tanh, scale=0.5), [t_cT], "c_tanh")
        t2 = put("dve", lambda e: e.tensor_scalar(cU[:], cT[:], 0.5, None, ALU.mult), [t_cT], "c_half")
        t_cS = put("dve", lambda e: e.scalar_tensor_tensor(out=cS[:], in0=cS[:], scalar=1.0, in1=cU[:],
                                                           op0=ALU.add, op1=ALU.mult), [t, t2], "c_silu")

        state = {"mod": [], "lnb": [], "cols": [], "bv": [], "bo": [], "bq": [], "bk": [], "w": {},
                 "cfree": []}
        wfree = {n: [] for n in "qkvo"}
        yfree = {"yb": [], "sT": [], "t": [], "s": []}
        stored = {}

        def prep_cols(L):
            t = load(f"l_cols{L}", cols[:, 0:16], A[f"cols{L}"], [state["cols"], state["lnb"]])
            for kt_ in range(NC):
                tl = put("dve", lambda e, k=kt_: e.tensor_scalar(lnb_b[:, k, :], ident[:], 0.0, cols[:, 4 + k:5 + k],
                                                                ALU.mult, ALU.add),
                         [t, t_id, state["lnb"], yfree["t"], yfree["s"]], "lnb_b")
            state["cols_in"], state["lnb_in"] = t, tl
            state["cols"], state["lnb"] = [tl], []
            yield

        def prep_w(L, n):
            fold = n != "o"
            i, bank, bw = work.take() if fold else (None, None, [])
            for kt_ in range(NC):
                j, raw, rw = wr.take()
                tr = load(f"l_w{j}", raw[:], A[f"W{n}{L}"][kt_ * 128:(kt_ + 1) * 128, :], rw)
                sc = cols[:, kt_:kt_ + 1] if fold else 1.0
                hi, lo = Wh[n][:, kt_, :], Wl[n][:, kt_, :]
                th = put("act", lambda e, a=hi, r=raw, s=sc: e.activation(a, r[:], ACT.Identity, scale=s),
                         [tr, state["cols_in"], wfree[n]], f"w_hi")
                tl = put("dve", lambda e, a=lo, h=hi, r=raw, s=sc: e.scalar_tensor_tensor(
                    out=a, in0=r[:], scalar=s, in1=h.bitcast(F32), op0=ALU.mult, op1=ALU.subtract),
                    [tr, th, state["cols_in"], wfree[n]], "w_lo")
                if fold:
                    tm = put("pe", lambda e, k=kt_, r=raw, b_=bank: e.matmul(
                        b_[:], lnb_b[:, k, :], r[:], start=(k == 0), stop=(k == NC - 1)),
                        [tr, state["lnb_in"], bw], "w_bias")
                    wr.release(j, th, tl, tm)
                else:
                    wr.release(j, th, tl)
                yield
            wfree[n] = []
            state["w"][n] = [th, tl]
            state["cols"] += [th, tl]
            if not fold:
                tb_ = load(f"l_bo", boB[:], A[f"bo{L}"].partition_broadcast(128), [state["bo"]])
                state["bo_in"], state["bo"] = tb_, []
                return
            state["lnb"] += [tm]
            dst = bvB if n == "v" else bqB
            if n == "v" or (n == "q" and L == 0):
                tb_ = load(f"l_b{n}", dst[:], A[f"b{n}{L}"].partition_broadcast(128), [state["b" + n]])
                ta = put("dve", lambda e, d=dst, b_=bank: e.tensor_tensor(d[:], b_[:], d[:], ALU.add),
                         [tb_, tm], "b_row")
                work.release(i, ta)
                state["b" + n + "_in"], state["b" + n] = ta, []
            else:
                col = bqc if n == "q" else bkc
                j, raw, rw = wr.take()
                tb_ = load(f"l_w{j}", raw[:], A[f"b{n}{L}"].partition_broadcast(128), rw)
                ta = put("dve", lambda e, r=raw, b_=bank: e.tensor_tensor(r[:], b_[:], r[:], ALU.add),
                         [tb_, tm], "b_row")
                work.release(i, ta)
                for c in range(NC):
                    td = put("dve", lambda e, r=raw, c=c: e.tensor_tensor(
                        r[:, c * 128:(c + 1) * 128], r[:, c * 128:(c + 1) * 128], ident[:], ALU.mult),
                        [ta, t_id], "b_diag")
                tc = put("dve", lambda e, r=raw, k=col: e.tensor_reduce(
                    k[:], r[:].rearrange("p (c n) -> p c n", c=NC), AX.X, ALU.add),
                    [td, state["b" + n]], "b_col")
                wr.release(j, tc)
                state["b" + n + "_in"], state["b" + n] = tc, []
            yield

        def prep_mod(L):
            for half in range(2):
                i, bank, bw = work.take()
                for k in range(8):
                    j, raw, rw = wr.take()
                    tr = load(f"l_w{j}", raw[:], A[f"We{L}"][k * 128:(k + 1) * 128, half * 512:(half + 1) * 512], rw)
                    tm = put("pe", lambda e, k=k, r=raw, b_=bank: e.matmul(
                        b_[0:B, :], cS[:, k, :], r[:], start=(k == 0), stop=(k == 7)), [tr, t_cS, bw], "e_mm")
                    wr.release(j, tm)
                    yield
                j, raw, rw = wr.take()
                tb_ = load(f"l_w{j}", raw[0:B, :], A[f"be{L}"][half * 512:(half + 1) * 512].partition_broadcast(B), rw)
                ta = put("dve", lambda e, r=raw, b_=bank: e.tensor_tensor(r[0:B, :], b_[0:B, :], r[0:B, :], ALU.add),
                         [tb_, tm], "e_row")
                work.release(i, ta)
                i, bank, bw = work.take()
                for c in range(NC):
                    tt = put("pe", lambda e, c=c, r=raw, b_=bank: e.transpose(
                        b_[:, c * B:(c + 1) * B], r[0:B, c * 128:(c + 1) * 128], ident[0:B, 0:B]),
                        [ta, t_id, bw], "e_tr")
                wr.release(j, tt)
                src = bank[:, 0:NC * B].rearrange("p (c b) -> p c b", c=NC)
                if half == 0:
                    t1 = put("dve", lambda e, s=src: e.tensor_scalar(mod[:, 0], s, 1.0, 0.5, ALU.add, ALU.mult),
                             [tt, state["mod"]], "e_mod")
                    work.release(i, t1)
                else:
                    for c in range(NC):
                        t2 = put("dve", lambda e, c=c, s=src: e.tensor_scalar(
                            mod[:, 1, c, :], s[:, c, :], 0.5, None, ALU.mult), [tt, state["mod"]], "e_mod")
                    work.release(i, t2)
                    for c in range(NC):
                        t3 = put("dve", lambda e, c=c: e.scalar_tensor_tensor(
                            out=mod[:, 1, c, :], in0=mod[:, 0, c, :], scalar=cols[:, 12 + c:13 + c],
                            in1=mod[:, 1, c, :], op0=ALU.mult, op1=ALU.add), [t1, t2, state["cols_in"]], "e_mod")
                    for c in range(NC):
                        t3 = put("dve", lambda e, c=c: e.tensor_scalar(
                            mod[:, 0, c, :], mod[:, 0, c, :], cols[:, 8 + c:9 + c], None, ALU.mult),
                            [t3, state["cols_in"]], "e_mod")
                    state["mod_in"], state["mod"] = t3, []
                    state["cols"] += [t3]
                yield

        lnpar = [0]
        lnfree = {0: [], 1: []}

        def norm(src, dst, tin, tfree, nm_):
            p = lnpar[0] % 2
            lnpar[0] += 1
            for t in range(NT):
                ta = put("dve", lambda e, t=t: e.bn_stats(st[:, p, t, :], src[:, t, :]), [tin[t]], "ln_st")
            for t in range(NT):
                tg = put("dve", lambda e, t=t: e.bn_aggr(mv[:, p, t, :], st[:, p, t, :]),
                         [(ta[0], ta[1] - NT + 1 + t), lnfree[p]], "ln_mv")
            tv = put("dve", lambda e: e.tensor_scalar(ve[:, p, :], mv[:, p, :, 1], EPS, None, ALU.add), [tg], "ln_ve")
            tr = put("pool", lambda e: e.tensor_tensor(rs[:, p, :], ve[:, p, :], mhalf[:], ALU.pow), [tv, t_mh], "ln_rs")
            tn = put("dve", lambda e: e.scalar_tensor_tensor(out=nm[:, p, :], in0=mv[:, p, :, 0], scalar=-1.0,
                                                             in1=rs[:, p, :], op0=ALU.mult, op1=ALU.mult),
                     [tr, tg], "ln_nm")
            res = []
            for t in range(NT):
                res.append(put("pool", lambda e, t=t: e.tensor_scalar(
                    dst[:, t, :], src[:, t, :], rs[:, p, t:t + 1], nm[:, p, t:t + 1], ALU.mult, ALU.add),
                    [tn, tr, tfree], nm_))
            lnfree[p] = [res[-1]]
            return res

        def turn(bank, srcs, waits, name):
            for t, s in enumerate(srcs):
                r = put("pe", lambda e, t=t, s=s: e.transpose(bank[:, t * 128:(t + 1) * 128], s, ident[:]),
                        [waits, t_id], name)
            return r

        def product(bank, lh, ll, rh, rl, waits, name):
            for k in range(NC):
                def f(e, k=k):
                    e.matmul(bank[:], lh(k), rh(k), start=(k == 0), stop=False)
                    e.matmul(bank[:], lh(k), rl(k), start=False, stop=False)
                    return e.matmul(bank[:], ll(k), rh(k), start=False, stop=(k == NC - 1))
                r = put("pe", f, waits, name)
                yield r

        xfree = {"xin": [], "xn": [], "xT": []}

        def load_x(L, b, xtick):
            src = A["x"] if L == 0 else x1d
            xfree["in", L, b] = [load(f"l_x{t}", xin[:, t, :], src[b, t * 128:(t + 1) * 128, :],
                                      [xfree["xin"], xtick]) for t in range(NT)]

        def stage_x(L, b):
            tn = norm(xin, xin, xfree["in", L, b], [], "xn")
            yield
            for c in range(NC):
                i, bank, bw = work.take()
                tt = turn(bank, [xin[:, t, c * 128:(c + 1) * 128] for t in range(NT)], [tn, bw], "xn_tr")
                th = put("act", lambda e, c=c, b_=bank: e.copy(xTh[:, c, :], b_[:]), [tt, xfree["xT"]], "xT_hi")
                tl = put("dve", lambda e, c=c, b_=bank: e.tensor_tensor(
                    xTl[:, c, :], b_[:], xTh[:, c, :].bitcast(F32), ALU.subtract), [tt, th, xfree["xT"]], "xT_lo")
                work.release(i, th, tl)
                yield
            xfree["xin"] = [tt]
            if b + 1 < B:
                load_x(L, b + 1, stored.get(b + 1, []))
            state["xT_in"] = [th, tl]
            state["xT_use"] = []

        def channel_major(n, g):
            return (lambda k: Wh[n][:, k, g * 128:(g + 1) * 128], lambda k: Wl[n][:, k, g * 128:(g + 1) * 128],
                    lambda k: xTh[:, k, :], lambda k: xTl[:, k, :])

        def token_major(n, t):
            return (lambda k: xTh[:, k, t * 128:(t + 1) * 128], lambda k: xTl[:, k, t * 128:(t + 1) * 128],
                    lambda k: Wh[n][:, k, :], lambda k: Wl[n][:, k, :])


        def stage_y(L, b, ty):
            xsrc = A["x"] if L == 0 else x1d
            bk = aux2 if L == 0 else work
            tn = norm(yb, yb, ty, [], "yn")
            yield
            tsh, tsl = None, None
            for c in range(NC):
                i, bank, bw = bk.take()
                tt = turn(bank, [yb[:, t, c * 128:(c + 1) * 128] for t in range(NT)], [tn, bw], "yn_tr")
                ta = put("act", lambda e, c=c, b_=bank: e.activation(
                    tb[:], b_[:], ACT.Tanh, scale=mod[:, 0, c, b:b + 1], bias=mod[:, 1, c, b:b + 1]),
                    [tt, state["mod_in"], yfree["t"]], "y_tanh")
                tu = put("dve", lambda e, c=c, b_=bank: e.tensor_scalar(
                    ub[:], b_[:], mod[:, 0, c, b:b + 1], mod[:, 1, c, b:b + 1], ALU.mult, ALU.add),
                    [tt, ta, state["mod_in"], yfree["s"]], "y_u")
                bk.release(i, ta, tu)
                tsf = put("dve", lambda e: e.scalar_tensor_tensor(out=ub[:], in0=tb[:], scalar=1.0, in1=ub[:],
                                                                 op0=ALU.add, op1=ALU.mult),
                          [ta, tu, yfree["s"]], "y_s")
                yfree["t"] = [tsf]
                tsh = put("pool", lambda e, c=c: e.tensor_scalar(sTh[:, c, :], ub[:], 1.0, 0.0, ALU.mult, ALU.add),
                          [tsf, yfree["sT"]], "s_hi")
                tsl = put("pool", lambda e, c=c: e.tensor_tensor(sTl[:, c, :], ub[:], sTh[:, c, :].bitcast(F32),
                                                                 ALU.subtract), [tsf, tsh, yfree["sT"]], "s_lo")
                yfree["s"] = [tsl]
                yield
            yfree["yb"] = [tt]
            state["mod"] = [ta, tu]
            outs = []
            for t in range(NT):
                j, xt, xw = wr.take()
                tx = load(f"l_w{j}", xt[:], xsrc[b, t * 128:(t + 1) * 128, :], xw)
                tx = put("pool", lambda e, x=xt: e.tensor_tensor(x[:], x[:], boB[:], ALU.add),
                         [tx, state["bo_in"]], "xb")
                i, bank, bw = bk.take()
                for tm in product(bank, lambda k, t=t: sTh[:, k, t * 128:(t + 1) * 128],
                                  lambda k, t=t: sTl[:, k, t * 128:(t + 1) * 128],
                                  lambda k: Wh["o"][:, k, :], lambda k: Wl["o"][:, k, :],
                                  [tsh, tsl, state["w"]["o"], bw], "o_mm"):
                    yield
                to = put("dve", lambda e, x=xt, b_=bank: e.tensor_tensor(x[:], b_[:], x[:], ALU.add), [tm, tx], "o_add")
                bk.release(i, to)
                dst = x1d if L == 0 else out
                tst = load(f"st{j}", dst[b, t * 128:(t + 1) * 128, :], xt[:], [to])
                wr.release(j, tst)
                outs.append(tst)
            state["bo"] = [tx]
            yfree["sT"] = [tm]
            wfree["o"] = [tm]
            if L == 0:
                stored[b] = outs
            yield

        f0 = {"ET": [], "E": [], "v": [], "eq": [], "A": [], "qs": {0: [], 1: []}, "ks": {0: [], 1: []}}
        za = put("dve", lambda e: e.memset(Ah[:].bitcast(F32), 0.0), sig="a_set")
        zb = put("dve", lambda e: e.memset(Al[:].bitcast(F32), 0.0), sig="a_set")
        put("dve", lambda e: e.memset(Ah[0:64, :, 128:129].bitcast(F32), 1.0), [za], sig="a_set")
        t_as = put("dve", lambda e: e.memset(Ah[64:128, :, 129:130].bitcast(F32), 1.0), [za], sig="a_set")
        r0 = {}

        def k0(b):
            p = b % 2
            im, mrow_, mw = mB.take()
            tm_ = load("l_mB", mrow_[:], A["m0"][b].partition_broadcast(128), mw)
            tmb = put("dve", lambda e, m=mrow_: e.tensor_scalar(m[:], m[:], 1.0, NEG, ALU.subtract, ALU.mult), [tm_], "mB")
            for g in range(NC):
                i, bank, bw = work.take()
                for tm in product(bank, *channel_major("k", g), [state["xT_in"], state["w"]["k"], bw], "k_mm"):
                    yield
                j, kb, kw = vt.take()
                tk = put("dve", lambda e, k=kb, b_=bank, m=mrow_, g=g: e.tensor_tensor_reduce(
                    k[:], b_[:], m[:], 1.0, -3.0e38, ALU.add, ALU.max, kmx[:, p, g:g + 1]),
                    [tm, tmb, kw, f0["ks"][p]], "k_max")
                work.release(i, tk)
                t1 = put("dve", lambda e, g=g: e.tensor_tensor(kmb[:, p, g:g + 1], kmx[:, p, g:g + 1],
                                                               bkc[:, g:g + 1], ALU.add), [tk, state["bk_in"]], "k_mb")
                t1 = put("dve", lambda e, g=g: e.tensor_tensor(knb[:, p, g:g + 1], bkc[:, g:g + 1],
                                                               kmb[:, p, g:g + 1], ALU.subtract), [t1], "k_mb")
                te = put("act", lambda e, k=kb, g=g: e.activation(ET[:, g, :], k[:], ACT.Exp,
                                                                  bias=knb[:, p, g:g + 1],
                                                                  accum_out=ksm[:, p, g:g + 1]),
                         [tk, t1, f0["ET"], f0["ks"][p]], "k_exp")
                vt.release(j, te)
                yield
            mB.release(im, tk)
            wfree["k"] = [tm]
            state["bk"] = [t1]
            r0["ET", b] = [te]
            r0["krc", b] = put("dve", lambda e: e.reciprocal(krc[:, p, :], ksm[:, p, :]), [te, f0["ks"][p]], "k_rc")

        def v0(b):
            for t in range(NT):
                i, bank, bw = work.take()
                for tm in product(bank, *token_major("v", t), [state["xT_in"], state["w"]["v"], bw], "v_mm"):
                    yield
                j, vb, vw = vt.take()
                ta = put("dve", lambda e, v=vb, b_=bank: e.tensor_tensor(v[:], b_[:], bvB[:], ALU.add),
                         [tm, state["bv_in"], vw], "v_add")
                work.release(i, ta)
                th = put("act", lambda e, v=vb, t=t: e.activation(vh[:, t, :], v[:], ACT.Identity,
                                                                  scale=mk[:, b, t:t + 1]), [ta, t_mk, f0["v"]], "v_hi")
                tl = put("dve", lambda e, v=vb, t=t: e.scalar_tensor_tensor(
                    out=vl[:, t, :], in0=v[:], scalar=mk[:, b, t:t + 1], in1=vh[:, t, :].bitcast(F32),
                    op0=ALU.mult, op1=ALU.subtract), [ta, th, f0["v"]], "v_lo")
                vt.release(j, th, tl)
                yield
            wfree["v"] = [tm]
            state["bv"] = [ta]
            r0["v", b] = [th, tl]

        def q0(b):
            for t in range(NT):
                i, bank, bw = work.take()
                for tm in product(bank, *token_major("q", t), [state["xT_in"], state["w"]["q"], bw], "q_mm"):
                    yield
                j, qb, qw = vt.take()
                ta = put("dve", lambda e, v=qb, b_=bank: e.tensor_tensor(v[:], b_[:], bqB[:], ALU.add),
                         [tm, state["bq_in"], qw], "q_add")
                work.release(i, ta)
                v3 = qb[:].rearrange("p (h d) -> p h d", h=H0)
                tx = put("dve", lambda e, v=v3, t=t: e.tensor_reduce(qmx[:, t % 2, :], v, AX.X, ALU.max),
                         [ta, f0["qs"][t % 2]], "q_max")
                tsb = put("pool", lambda e, v=v3, t=t: e.tensor_tensor(
                    v, v, qmx[:, t % 2, :].unsqueeze(2).to_broadcast([128, H0, 64]), ALU.subtract), [tx], "q_sub")
                f0["qs"][t % 2] = [tsb]
                te = put("act", lambda e, v=qb, t=t: e.activation(eq[:, t, :], v[:], ACT.Exp), [tsb, f0["eq"]], "q_exp")
                vt.release(j, te)
                yield
            wfree["q"] = [tm]
            state["bq"] = [ta]
            xfree["xT"] = [tm]
            r0["eq", b] = [te]

        def turn_e0(b):
            for t in range(NT):
                i, bank, bw = aux.take()
                tt = turn(bank, [ET[:, g, t * 128:(t + 1) * 128] for g in range(NC)], [r0["ET", b], bw], "E_tr")
                th = put("act", lambda e, t=t, b_=bank: e.copy(Eh[:, t, :], b_[:]), [tt, f0["E"]], "E_hi")
                tl = put("dve", lambda e, t=t, b_=bank: e.tensor_tensor(
                    El[:, t, :], b_[:], Eh[:, t, :].bitcast(F32), ALU.subtract), [tt, th, f0["E"]], "E_lo")
                aux.release(i, th, tl)
                yield
            f0["ET"] = [tt]
            r0["E", b] = [th, tl]

        def state0(b):
            p = b % 2
            i, bank, bw = aux.take()
            for g in range(NC):
                def f(e, g=g, b_=bank):
                    n = slice(g * 128, (g + 1) * 128)
                    for t in range(NT):
                        e.matmul(b_[:, n], Eh[:, t, n], vh[:, t, n], start=(t == 0), stop=False)
                        e.matmul(b_[:, n], Eh[:, t, n], vl[:, t, n], start=False, stop=False)
                        r = e.matmul(b_[:, n], El[:, t, n], vh[:, t, n], start=False, stop=(t == NT - 1))
                    return r
                ta = put("pe", f, [r0["E", b], r0["v", b], bw], "att")
                yield
            f0["E"], f0["v"] = [ta], [ta]
            b3 = bank[:].rearrange("p (g n) -> p g n", g=NC)
            tz = []
            for h in range(2):
                r_ = slice(64 * h, 64 * h + 64)
                tf = put("dve", lambda e, r_=r_, h=h, b3=b3: e.tensor_tensor(
                    Af[r_], b3[r_, :, 64 * h:64 * h + 64],
                    krc[r_, p, :].unsqueeze(2).to_broadcast([64, NC, 64]), ALU.mult),
                    [ta, r0["krc", b], f0["A"]], "A_sc")
                tz.append(tf)
                th2 = put("act", lambda e, r_=r_, h=h: e.copy(Ah[r_, :, 64 * h:64 * h + 64], Af[r_]),
                          [tf, f0["A"], t_as], "A_hi")
                tl2 = put("dve", lambda e, r_=r_, h=h: e.tensor_tensor(
                    Al[r_, :, 64 * h:64 * h + 64], Af[r_], Ah[r_, :, 64 * h:64 * h + 64].bitcast(F32), ALU.subtract),
                    [tf, th2, f0["A"]], "A_lo")
            aux.release(i, *tz)
            f0["ks"][p] = [tz[-1]]
            r0["A", b] = [th2, tl2]
            f0["Aw"] = [tl2]
            yield

        def y0(b):
            for g in range(NC):
                i, bank, bw = aux.take()
                tt = turn(bank, [eq[:, t, g * 128:(g + 1) * 128] for t in range(NT)], [r0["eq", b], bw], "q_tr")
                jh, ah, wh_ = qh.take()
                jl, al, wl_ = ql.take()
                th = put("act", lambda e, a=ah, b_=bank: e.copy(a[:], b_[:]), [tt, wh_], "qT_hi")
                tl = put("dve", lambda e, a=al, h=ah, b_=bank: e.tensor_tensor(
                    a[:], b_[:], h[:].bitcast(F32), ALU.subtract), [tt, th, wl_], "qT_lo")
                aux.release(i, th, tl)
                yield
                for half in range(2):
                    i, bank, bw = aux2.take()

                    def f(e, half=half, g=g, b_=bank, ah=ah, al=al):
                        for u in range(2):
                            t = 2 * half + u
                            n, o = slice(t * 128, (t + 1) * 128), b_[:, u * 130:(u + 1) * 130]
                            e.matmul(o, ah[:, n], Ah[:, g, :], start=True, stop=False)
                            e.matmul(o, ah[:, n], Al[:, g, :], start=False, stop=False)
                            r = e.matmul(o, al[:, n], Ah[:, g, :], start=False, stop=True)
                        return r
                    tm = put("pe", f, [th, tl, r0["A", b], bw], "y_mm")
                    y3 = bank[:, 0:260].rearrange("p (u n) -> p u n", u=2)
                    tr = put("dve", lambda e, y3=y3: e.reciprocal(
                        yrc[:].rearrange("p (u h) -> p u h", u=2), y3[:, :, 128:130]),
                        [tm, f0.get("yrc", [])], "y_rc")
                    o4 = yb[:, 2 * half:2 * half + 2, g * 128:(g + 1) * 128]
                    for u in range(2):
                        ty = put("dve", lambda e, u=u, o4=o4, y3=y3: e.tensor_tensor(
                            o4[:, u, :].rearrange("p (h d) -> p h d", h=2),
                            y3[:, u, 0:128].rearrange("p (h d) -> p h d", h=2),
                            yrc[:, 2 * u:2 * u + 2].unsqueeze(2).to_broadcast([128, 2, 64]), ALU.mult),
                            [tr, yfree["yb"]], "y_sc")
                    aux2.release(i, ty)
                    f0["yrc"] = [ty]
                    yield
                qh.release(jh, tm)
                ql.release(jl, tm)
            f0["eq"] = [tt]
            f0["A"] = [tm]
            r0["y", b] = [ty] * NT

        s1 = {"stack": {0: [], 1: []}, "qsg": [], "ksg": [], "v": [], "Ps": [], "yT": [], "dT": [], "nx": {0: [], 1: []},
              "mr": [], "rd": [], "nxd": [], "pv": [], "den": []}
        r1 = {}
        mf = {}

        def begin1(after):
            mrow, mrh, mrl = yT[0:B, :], sg["qh"][0:B, :], sg["ql"][0:B, :]
            tm_ = load("l_mr", mrow, A["m1"], after)
            t1 = put("dve", lambda e: e.tensor_scalar(mrow, mrow, 1.0, NEG, ALU.subtract, ALU.mult), [tm_], "mr")
            t2 = put("act", lambda e: e.copy(mrh, mrow), [t1, after], "mr_hi")
            t3 = put("dve", lambda e: e.tensor_tensor(mrl, mrow, mrh.bitcast(F32), ALU.subtract),
                     [t1, t2, after], "mr_lo")
            mf["m"] = [load("l_mrs0", md[0], mrh, [t2]), load("l_mrs1", md[1], mrl, [t3])]
            s1["qsg"], s1["yT"] = mf["m"], [t2, t3]
            for i in range(2):
                ta = put("dve", lambda e, i=i: e.memset(Qs[i][RM:RM + 32].bitcast(F32), 1.0), after, "st_set")
                tb_ = put("dve", lambda e, i=i: e.memset(Ks[i][RM:RM + 32].bitcast(F32), 1.0), after, "st_set")
                s1["stack"][i] = [ta, tb_]
            mf["after"] = after
            yield

        def v1(b):
            for t in range(NT):
                i, bank, bw = work.take()
                for tm in product(bank, *token_major("v", t), [state["xT_in"], state["w"]["v"], bw], "v_mm"):
                    yield
                j, vb, vw = vt.take()
                ta = put("dve", lambda e, v=vb, b_=bank: e.tensor_tensor(v[:], b_[:], bvB[:], ALU.add),
                         [tm, state["bv_in"], vw], "v_add")
                work.release(i, ta)
                tv = put("pool", lambda e, v=vb, t=t: e.tensor_scalar(
                    vf[:, t, :], v[:], mk[:, b, t:t + 1], 1.0, ALU.mult, ALU.mult),
                    [ta, t_mk1, s1["v"], mf["after"]], "v_out")
                vt.release(j, tv)
                yield
            wfree["v"] = [tm]
            r1["v", b] = [tv]

        def qk1(b, g):
            par = (4 * b + g) % 2
            free = [s1["stack"][par], mf["after"]]
            ts = []
            for n, S, rows in (("q", Qs[par], ("h", "h", "l")), ("k", Ks[par], ("h", "l", "h"))):
                col = bqc if n == "q" else bkc
                i, bank, bw = work.take()
                for tm in product(bank, *channel_major(n, g), [state["xT_in"], state["w"][n], bw], n + "_mm"):
                    yield
                hi, lo = sg[n + "h"], sg[n + "l"]
                th = put("act", lambda e, a=hi, b_=bank, c=col: e.activation(
                    a[:], b_[:], ACT.Identity, bias=c[:, g:g + 1]), [tm, s1[n + "sg"], mf["after"]], n + "_hi")
                tl = put("dve", lambda e, a=lo, h=hi, b_=bank, c=col: e.scalar_tensor_tensor(
                    out=a[:], in0=b_[:], scalar=c[:, g:g + 1], in1=h[:].bitcast(F32),
                    op0=ALU.add, op1=ALU.subtract), [tm, th, s1[n + "sg"], mf["after"]], n + "_lo")
                work.release(i, th, tl)
                for r, part in enumerate(rows):
                    src = hi if part == "h" else lo
                    for j in range(4):
                        td = load(f"stk{n}{par}", S[32 * r:32 * r + 32, j, :], src[32 * j:32 * j + 32, :],
                                  [th if part == "h" else tl, free])
                s1[n + "sg"] = [td]
                ts.append(td)
            for r, src in ((RM, md[0]), (RM + 1, md[1])):
                for j in range(4):
                    td = load(f"stm{par}", Ks[par][r:r + 1, j, :], src[b:b + 1, :], [mf["m"], free])
            ts.append(td)
            r1["stack", b, g] = ts
            if g == NG - 1:
                xfree["xT"] = [tm]
            yield

        def max1(b, g):
            par = (4 * b + g) % 2
            for j in range(4):
                for t in range(NT):
                    i, bank, bw = sbank.take()
                    tm = put("pe", lambda e, j=j, t=t, b_=bank: e.matmul(
                        b_[:], Qs[par][0:RX, j, t * 128:(t + 1) * 128], Ks[par][0:RX, j, :], start=True, stop=True),
                        [r1["stack", b, g], bw], "S")
                    tx = put("dve", lambda e, j=j, t=t, b_=bank: e.tensor_reduce(
                        nx[:, par, j * NT + t:j * NT + t + 1], b_[:], AX.X, ALU.max, negate=True),
                        [tm, s1["nx"][par], mf["after"]], "S_max")
                    sbank.release(i, tx)
                    yield
            i, bank, bw = sbank.take()
            yield
            tt = put("pe", lambda e, b_=bank: e.transpose(b_[0:16, 0:128], nx[:, par, :], ident[:]), [tx, bw], "nx_tr")
            th = put("act", lambda e, b_=bank: e.copy(nxh[:], b_[0:16, 0:128]), [tt, s1["nxd"]], "nx_hi")
            tl = put("dve", lambda e, b_=bank: e.tensor_tensor(
                nxl[:], b_[0:16, 0:128], nxh[:].bitcast(F32), ALU.subtract),
                [tt, th, s1["nxd"]], "nx_lo")
            sbank.release(i, th, tl)
            s1["nx"][par] = [tt]
            for r, src in ((RX, nxh), (RX + 1, nxl)):
                td0, td = (td if r > RX else None), load(f"nxd{par}", Qs[par][r:r + 1, :, :].rearrange("p j (t n) -> p (j t) n", t=NT),
                          src[:], [th, tl, tm])
            s1["nxd"] = [td0, td]
            r1["nx", b, g] = [td]
            r1["nx_rd", b, g] = [tm]
            yield

        def att1(b, g):
            par = (4 * b + g) % 2
            PV, DEN = ps[6], ps[7]
            prev = None

            def pv(m, pb, te):
                def f(e, m=m, pb=pb):
                    for j in range(4):
                        h = 4 * g + j
                        r = e.matmul(PV[32 * j:32 * j + 32, :], vf[:, m, h * 32:(h + 1) * 32], pb[:, j, :],
                                     start=(m == 0), stop=(m == NT - 1))
                    return r
                return put("pe", f, [te, r1["v", b], s1["pv"]], "PV")

            tps = None
            for m in range(NT + 1):
                if m < NT:
                    ip, pb, pw = Pb.take()
                    te = []
                    for j in range(4):
                        i, bank, bw = tbank.take()
                        tm = put("pe", lambda e, j=j, m=m, b_=bank: e.matmul(
                            b_[:], Ks[par][0:RE, j, m * 128:(m + 1) * 128], Qs[par][0:RE, j, :], start=True, stop=True),
                            [r1["nx", b, g], bw], "ST")
                        te.append(put("act", lambda e, j=j, b_=bank, pb=pb: e.activation(
                            pb[:, j, :], b_[:], ACT.Exp), [tm, pw, mf["after"]], "P"))
                        tbank.release(i, te[-1])
                        yield
                if prev is not None:
                    pm, pip, ppb, pte = prev
                    tpv = pv(pm, ppb, pte)
                    yield
                    if pm == 0:
                        ik, pk, tk = pip, ppb, tpv
                    else:
                        eng = "dve" if pm == 1 else "pool"
                        for j in range(4):
                            tps = put(eng, lambda e, j=j, a=pk, c=ppb: e.tensor_tensor(
                                a[:, j, :], a[:, j, :], c[:, j, :], ALU.add), [pte, tk, tps], f"Ps_{eng}")
                        Pb.release(pip, tpv, tps)
                if m < NT:
                    prev = (m, ip, pb, te)
            s1["stack"][par] = [tm]
            s1["v_last"] = [tpv]

            def f(e):
                for j in range(4):
                    r = e.matmul(DEN[32 * j:32 * j + 32, :], ones[:, 0:32], pk[:, j, :], start=True, stop=True)
                return r
            yield
            tcy = put("act", lambda e: e.copy(yT[:], PV[:]), [tpv, s1["yT"], mf["after"]], "yT")
            yield
            yield
            td = put("pe", f, [tps, s1["den"]], "den")
            Pb.release(ik, td)
            tcd = put("act", lambda e: e.copy(dT[:], DEN[:]), [td, s1["dT"], mf["after"]], "dT")
            yield
            ba, bb = PV, DEN
            ta = turn(ba, [yT[:, t * 128:(t + 1) * 128] for t in range(NT)], [tcy], "y1_tr")
            s1["yT"] = [ta]
            yield
            tb_ = turn(bb, [dT[:, t * 128:(t + 1) * 128] for t in range(NT)], [tcd], "d1_tr")
            s1["dT"] = [tb_]
            tr = put("dve", lambda e, bb=bb: e.reciprocal(
                rd[:], bb[:].rearrange("p (t j l) -> p t j l", t=NT, j=4)[:, :, :, 0]), [tb_, s1["rd"], mf["after"]], "rd")
            s1["den"] = [tr]
            for t in range(NT):
                ty = put("dve", lambda e, t=t, ba=ba: e.tensor_tensor(
                    yb[:, t, g * 128:(g + 1) * 128].rearrange("p (j l) -> p j l", j=4),
                    ba[:, t * 128:(t + 1) * 128].rearrange("p (j l) -> p j l", j=4),
                    rd[:, t, :].unsqueeze(2).to_broadcast([128, 4, 32]), ALU.mult), [ta, tr, yfree["yb"]], "y1")
            s1["pv"] = [ty]
            s1["rd"] = [ty]
            r1["y", b, g] = [ty]
            if g == NG - 1:
                s1["v"] = [tpv]
            yield

        def run(*gs):
            for _ in chain(*gs):
                pass

        load_x(0, 0, [])
        run(prep_cols(0), stage_x(0, 0))
        run(prep_w(0, "k"))
        for b in range(B + 1):
            more = b < B
            interleave((k0(b) if more else None, 20.0), (y0(b - 1) if b >= 1 else None, 12.0))
            prev = stage_y(0, b - 1, r0["y", b - 1]) if b >= 1 else None
            first = b == 0
            interleave((chain(prep_w(0, "v") if first else None, v0(b) if more else None), 20.0),
                       (turn_e0(b) if more else None, 4.0), (part(prev, 11), 11.0))
            interleave((chain(prep_w(0, "q") if first else None, q0(b) if more else None,
                              prep_w(0, "o") if first else None, prep_mod(0) if first else None,
                              stage_x(0, b + 1) if b + 1 < B else None), 25.0),
                       (state0(b) if more else None, 6.0), (prev, 12.0))
        after = [tick for tick in [f0["A"], f0["E"], f0["v"], f0["eq"], f0["ET"], f0["yrc"], f0["ks"][0], f0["ks"][1]]]
        after = [list(flat(after)), list(flat([r0["krc", B - 1], f0["Aw"], state["bq"], state["bk"]]))]
        after = [list(flat(after))]

        t_mk1 = load("l_mk1", mk[:], A["mk1"], [f0["v"]])
        load_x(1, 0, stored[0])
        run(begin1(after), prep_cols(1), prep_w(1, "k"), prep_w(1, "q"), prep_w(1, "v"), prep_w(1, "o"), prep_mod(1))
        free_w = dict(wfree)
        last_psum = [w for r in (aux, aux2) for _, w in r.free]
        for r in (sbank, tbank):
            r.free = [(i, last_psum) for i in range(2)]
        s1["pv"], s1["den"] = list(last_psum), list(last_psum)
        run(stage_x(1, 0), v1(0), qk1(0, 0), qk1(0, 1), max1(0, 0))
        seq = [(b, g) for b in range(B) for g in range(NG)]
        pend_y = None
        for n, (b, g) in enumerate(seq):
            nxt = seq[n + 1] if n + 1 < len(seq) else None
            nx2 = seq[n + 2] if n + 2 < len(seq) else None
            fill = []
            if g == 0 and b >= 1:
                fill.append(stage_y(1, b - 1, [[r1["y", b - 1, h] for h in range(NG)]] * NT))
            if g == 2 and b + 1 < B:
                fill.append(stage_x(1, b + 1))
            interleave((att1(b, g), 24.0), (max1(*nxt) if nxt else None, 18.0), (chain(*fill), 24.0))
            if g == NG - 1 and b + 1 < B:
                pass
            if g == NG - 1 and b + 1 < B:
                run(v1(b + 1))
            if nx2:
                run(qk1(*nx2))
        run(stage_y(1, B - 1, [[r1["y", B - 1, h] for h in range(NG)]] * NT))
        for j in range(2):
            c = Q.sem(f"st{j}")
            Q.q["sp"].append((lambda e: None, [(c, c.n)], None, 16))
        block = ctx.enter_context(nc.Block())

        @block.sync
        def _(e):
            Q.run("sp", e)

        @block.gpsimd
        def _(e):
            Q.run("pool", e)

        @block.scalar
        def _(e):
            Q.run("act", e)

        @block.vector
        def _(e):
            Q.run("dve", e)

        @block.tensor
        def _(e):
            Q.run("pe", e)


def kernel(**inputs):
    import numpy as np
    import concourse.bacc as bacc
    from concourse import mybir as mb
    from concourse.bass_utils import run_bass_kernel_spmd

    g = {k: np.asarray(v) for k, v in inputs.items()}

    def col(v):
        return v.reshape(NC, 128).T

    def mcol(m):
        return np.ascontiguousarray(m.reshape(B, NT, 128).transpose(2, 0, 1))

    P0, P1 = "L0_cond_", "L1_cond_"
    a = {
        "x": g["x"],
        "m0": g["mask_BxSx1_fk1"].reshape(B, T),
        "m1": g["mask_BxS_ff1"],
        "mk": mcol(g["mask_BxSx1_fk1"]),
        "mk1": mcol(g["mask_BxS_ff1"]),
        "cT": np.ascontiguousarray(g["cond_2048"].T.reshape(8, 128, B).transpose(1, 0, 2)),
        "cols0": np.concatenate([col(g[P0 + n]) for n in ("ln_w", "ln_b", "ln2_w", "ln2_b")], axis=1),
        "cols1": np.concatenate([col(g[P1 + n]) for n in ("norm_w", "norm_b", "sb_norm_w", "sb_norm_b")], axis=1),
        "Wq0": g[P0 + "Wq"], "bq0": g[P0 + "bq"], "Wk0": g[P0 + "Wk"], "bk0": g[P0 + "bk"],
        "Wv0": g[P0 + "Wv"], "bv0": g[P0 + "bv"], "We0": g[P0 + "W_emb"], "be0": g[P0 + "b_emb"],
        "Wo0": g[P0 + "W_out"], "bo0": g[P0 + "b_out"],
        "Wq1": g[P1 + "q_w"], "bq1": g[P1 + "q_b"], "Wk1": g[P1 + "k_w"], "bk1": g[P1 + "k_b"],
        "Wv1": g[P1 + "v_w"], "bv1": g[P1 + "v_b"], "We1": g[P1 + "emb_w"], "be1": g[P1 + "emb_b"],
        "Wo1": g[P1 + "out_w"], "bo1": g[P1 + "out_b"],
    }
    nc = bacc.Bacc("TRN2", target_bir_lowering=False, num_devices=1)
    arrays, aps = {}, {}
    for n, v in a.items():
        v = np.ascontiguousarray(v)
        arrays["in_" + n] = v
        aps[n] = nc.dram_tensor("in_" + n, v.shape, mb.dt.from_np(v.dtype), kind="ExternalInput").ap()
    out = nc.dram_tensor("out_0", (B, T, D), mb.dt.float32, kind="ExternalOutput").ap()
    cond_two_layers(nc, aps, out)
    r = run_bass_kernel_spmd(nc, [arrays], core_ids=[0])
    return r.results[0]["out_0"]
```

```python
from contextlib import ExitStack

import concourse.bass as bass
from concourse import mybir

ALU = mybir.AluOpType
ACT = mybir.ActivationFunctionType
AX = mybir.AxisListType
F32 = mybir.dt.float32
FR = mybir.dt.float32r

B, T, D, TE = 8, 512, 512, 1024
NT = T // 128
NC = D // 128
EPS = 1e-5
NEG = 1000000.0
H0, H1 = 8, 16
NG = 4
RM, RX, RE = 96, 98, 100



class Counter:

    def __init__(self, handle):
        self.h, self.n = handle, 0

    def add(self, k):
        self.n += k
        return (self, self.n)


class Queues:

    def __init__(self, nc, ctx):
        self.nc, self.ctx, self.sems = nc, ctx, {}
        self.q = {e: [] for e in ("pe", "act", "dve", "pool", "sp")}
        self.seen = {e: {} for e in self.q}

    def sem(self, name):
        if name not in self.sems:
            self.sems[name] = Counter(self.ctx.enter_context(self.nc.semaphore("s_" + name)))
        return self.sems[name]

    def put(self, eng, fn, waits=(), sig=None):
        need = []
        for w in flat(waits):
            if self.seen[eng].get(w[0], 0) < w[1]:
                self.seen[eng][w[0]] = w[1]
                need.append(w)
        s = self.sem(sig) if sig else None
        step = 16 if eng == "sp" else 1
        self.q[eng].append((fn, need, s, step))
        return s.add(step) if s else None

    def run(self, eng, e):
        for fn, need, s, step in self.q[eng]:
            for c, v in need:
                e.wait_ge(c.h, v)
            ins = fn(e)
            if s:
                ins.then_inc(s.h, step)


def flat(ws):
    for w in ws:
        if w is None:
            continue
        if isinstance(w, tuple):
            yield w
        else:
            yield from flat(w)


def raw32(ap):
    return ap.bitcast(F32) if ap.dtype == FR else ap


class Ring:

    def __init__(self, bufs):
        self.bufs = bufs
        self.free = [(i, []) for i in range(len(bufs))]

    def take(self):
        assert self.free, "taken again before its readers were queued"
        i, w = self.free.pop(0)
        return i, self.bufs[i], w

    def release(self, i, *ticks):
        self.free.append((i, list(ticks)))


def interleave(*gens):
    live = [[g, (b - a) / total, a] for g, total, a, b in gens if g is not None]
    while live:
        it = min(live, key=lambda x: x[2])
        try:
            it[2] += next(it[0]) * it[1]
        except StopIteration:
            live.remove(it)


def chain(*gens):
    for g in gens:
        if g is not None:
            yield from g


def cond_two_layers(nc, A, out):
    ctx = ExitStack()
    with ctx:
        Q = Queues(nc, ctx)
        put = Q.put

        def sb(name, shape, dt=F32, c=ctx):
            return c.enter_context(nc.sbuf_tensor(name, shape, dt))

        md = nc.dram_tensor("mask_scratch", [2, B, T], F32, kind="Internal").ap()
        qkd = nc.dram_tensor("stack_scratch", [2, 2, 2, 128, T], F32, kind="Internal").ap()
        x1d = nc.dram_tensor("x1_scratch", [B, T, D], F32, kind="Internal").ap()

        Wh = {n: sb("Wh_" + n, [128, NC, D], FR) for n in "qkvo"}
        Wl = {n: sb("Wl_" + n, [128, NC, D], FR) for n in "qkvo"}
        xin = sb("xin", [128, NT, D])
        xTh = sb("xTh", [128, NC, T], FR)
        xTl = sb("xTl", [128, NC, T], FR)
        yb = sb("yb", [128, NT, D])
        sTh = sb("sTh", [128, NC, T], FR)
        sTl = sb("sTl", [128, NC, T], FR)
        tb = sb("tb", [128, D])
        ub = sb("ub", [128, D])
        lnb_b = ub[:].rearrange("p (c n) -> p c n", c=NC)
        vt = Ring([sb("vt0", [128, D]), sb("vt1", [128, D])])
        wr = Ring([sb("wr0", [128, D]), sb("wr1", [128, D])])
        bvB = sb("bvB", [128, D])
        boB = sb("boB", [128, D])
        ident = sb("ident", [128, 128])
        ones = sb("ones", [128, 32])
        mhalf = sb("mhalf", [128, NT])
        cols = sb("cols", [128, 24])
        bqc = sb("bqc", [128, NC])
        bkc = sb("bkc", [128, NC])
        mk = sb("mk", [128, B, NT])
        mod = sb("mod", [128, 2, NC, B])
        cT = sb("cT", [128, 8, B])
        cS = sb("cS", [128, 8, B])
        cU = sb("cU", [128, 8, B])
        st = sb("st", [128, 2, NT, 6])
        mv = sb("mv", [128, 2, NT, 2])
        ve = sb("ve", [128, 2, NT])
        rs = sb("rs", [128, 2, NT])
        nm = sb("nm", [128, 2, NT])

        c0 = ExitStack()
        mB = Ring([sb("mB0", [128, T], c=c0)])
        ET = sb("ET", [128, NC, T], c=c0)
        Eh = sb("Eh", [128, NT, D], FR, c=c0)
        El = sb("El", [128, NT, D], FR, c=c0)
        vh = sb("vh", [128, NT, D], FR, c=c0)
        vl = sb("vl", [128, NT, D], FR, c=c0)
        eq = sb("eq", [128, NT, D], c=c0)
        qh = Ring([sb("qh0", [128, T], FR, c=c0), sb("qh1", [128, T], FR, c=c0)])
        ql = Ring([sb("ql0", [128, T], FR, c=c0), sb("ql1", [128, T], FR, c=c0)])
        bqB = sb("bqB", [128, D], c=c0)
        Af = sb("Af", [128, NC, 64], c=c0)
        Ah = sb("Ah", [128, NC, 130], FR, c=c0)
        Al = sb("Al", [128, NC, 130], FR, c=c0)
        qmx = sb("qmx", [128, 2, H0], c=c0)
        kmx = sb("kmx", [128, 2, NC], c=c0)
        kmb = sb("kmb", [128, 2, NC], c=c0)
        knb = sb("knb", [128, 2, NC], c=c0)
        ksm = sb("ksm", [128, 2, NC], c=c0)
        krc = sb("krc", [128, 2, NC], c=c0)
        yrc = sb("yrc", [128, 4], c=c0)
        c0.close()

        c1 = ctx
        Qs = [sb(f"Qs{i}", [128, 4, T], FR, c=c1) for i in range(2)]
        Ks = [sb(f"Ks{i}", [128, 4, T], FR, c=c1) for i in range(2)]
        sg = {n: sb("sg_" + n, [128, 2, T], FR, c=c1) for n in "qk"}
        vf = sb("vf", [128, NT, D], c=c1)
        Pb = Ring([sb(f"Pb{i}", [128, 4, T], c=c1) for i in range(3)])
        yT = sb("yT", [128, T], c=c1)
        dT = sb("dT", [128, T], c=c1)
        rd = sb("rd", [128, NT, NG, 4], c=c1)
        sel = sb("sel", [128, 36], c=c1)
        nx = sb("nx", [128, 2, 16], c=c1)
        nxh = sb("nxh", [16, 128], FR, c=c1)
        nxl = sb("nxl", [16, 128], FR, c=c1)

        ps = [ctx.enter_context(nc.psum_tensor(f"ps{i}", [128, 512], F32)) for i in range(8)]
        work = Ring([ps[0], ps[1]])
        aux = Ring([ps[2], ps[3], ps[4]])
        aux2 = Ring([ps[5], ps[6], ps[7]])
        sbank = Ring([ps[2], ps[3]])
        tbank = Ring([ps[4], ps[5]])
        PV, DEN = ps[6], ps[7]

        t_c = put("pool", lambda e: e.memset(ones[:], 1.0), sig="ones")
        t_c0 = put("pool", lambda e: e.memset(ident[:], 0.0), sig="const")
        t_id = put("pool", lambda e: e.affine_select(out=ident[:], in_=ident[:], compare_op=ALU.not_equal,
                                                     fill=1.0, base=0, pattern=[[-1, 128]],
                                                     channel_multiplier=1), [t_c0], sig="const")
        t_mh = put("pool", lambda e: e.memset(mhalf[:], -0.5), sig="const")

        def load(name, dst, src, waits=()):
            dst, src = raw32(dst), raw32(src)
            return put("sp", lambda e: e.dma_start(dst, src), waits, sig=name)

        t_mk = load("l_mk", mk[:], A["mk"])
        t_cT = load("l_cT", cT[:], A["cT"])

        t = put("act", lambda e: e.activation(cS[:], cT[:], ACT.Tanh, scale=0.5), [t_cT], "c_tanh")
        t2 = put("dve", lambda e: e.tensor_scalar(cU[:], cT[:], 0.5, None, ALU.mult), [t_cT], "c_half")
        t_cS = put("dve", lambda e: e.scalar_tensor_tensor(out=cS[:], in0=cS[:], scalar=1.0, in1=cU[:],
                                                           op0=ALU.add, op1=ALU.mult), [t, t2], "c_silu")

        state = {"mod": [], "lnb": [], "cols": [], "bv": [], "bo": [], "bq": [], "bk": [], "w": {},
                 "cfree": []}
        wfree = {n: [] for n in "qkvo"}
        yfree = {"yb": [], "sT": [], "t": [], "s": []}
        stored = {}

        def prep_cols(L):
            t = load(f"l_cols{L}", cols[:, 0:16], A[f"cols{L}"], [state["cols"], state["lnb"]])
            for kt_ in range(NC):
                tl = put("dve", lambda e, k=kt_: e.tensor_scalar(lnb_b[:, k, :], ident[:], 0.0, cols[:, 4 + k:5 + k],
                                                                ALU.mult, ALU.add),
                         [t, t_id, state["lnb"], yfree["t"], yfree["s"]], "lnb_b")
            state["cols_in"], state["lnb_in"] = t, tl
            state["cols"], state["lnb"] = [tl], []
            yield 0.5

        def prep_w(L, n):
            fold = n != "o"
            i, bank, bw = work.take() if fold else (None, None, [])
            for kt_ in range(NC):
                j, raw, rw = wr.take()
                tr = load(f"l_w{j}", raw[:], A[f"W{n}{L}"][kt_ * 128:(kt_ + 1) * 128, :], rw)
                sc = cols[:, kt_:kt_ + 1] if fold else 1.0
                hi, lo = Wh[n][:, kt_, :], Wl[n][:, kt_, :]
                th = put("act", lambda e, a=hi, r=raw, s=sc: e.activation(a, r[:], ACT.Identity, scale=s),
                         [tr, state["cols_in"], wfree[n]], f"w_hi")
                tl = put("dve", lambda e, a=lo, h=hi, r=raw, s=sc: e.scalar_tensor_tensor(
                    out=a, in0=r[:], scalar=s, in1=h.bitcast(F32), op0=ALU.mult, op1=ALU.subtract),
                    [tr, th, state["cols_in"], wfree[n]], "w_lo")
                if fold:
                    tm = put("pe", lambda e, k=kt_, r=raw, b_=bank: e.matmul(
                        b_[:], lnb_b[:, k, :], r[:], start=(k == 0), stop=(k == NC - 1)),
                        [tr, state["lnb_in"], bw], "w_bias")
                    wr.release(j, th, tl, tm)
                else:
                    wr.release(j, th, tl)
                yield 0.5
            wfree[n] = []
            state["w"][n] = [th, tl]
            state["cols"] += [th, tl]
            if not fold:
                tb_ = load(f"l_bo", boB[:], A[f"bo{L}"].partition_broadcast(128), [state["bo"]])
                state["bo_in"], state["bo"] = tb_, []
                return
            state["lnb"] += [tm]
            dst = bvB if n == "v" else bqB
            if n == "v" or (n == "q" and L == 0):
                tb_ = load(f"l_b{n}", dst[:], A[f"b{n}{L}"].partition_broadcast(128), [state["b" + n]])
                ta = put("dve", lambda e, d=dst, b_=bank: e.tensor_tensor(d[:], b_[:], d[:], ALU.add),
                         [tb_, tm], "b_row")
                work.release(i, ta)
                state["b" + n + "_in"], state["b" + n] = ta, []
            else:
                col = bqc if n == "q" else bkc
                j, raw, rw = wr.take()
                tb_ = load(f"l_w{j}", raw[:], A[f"b{n}{L}"].partition_broadcast(128), rw)
                ta = put("dve", lambda e, r=raw, b_=bank: e.tensor_tensor(r[:], b_[:], r[:], ALU.add),
                         [tb_, tm], "b_row")
                work.release(i, ta)
                for c in range(NC):
                    td = put("dve", lambda e, r=raw, c=c: e.tensor_tensor(
                        r[:, c * 128:(c + 1) * 128], r[:, c * 128:(c + 1) * 128], ident[:], ALU.mult),
                        [ta, t_id], "b_diag")
                tc = put("dve", lambda e, r=raw, k=col: e.tensor_reduce(
                    k[:], r[:].rearrange("p (c n) -> p c n", c=NC), AX.X, ALU.add),
                    [td, state["b" + n]], "b_col")
                wr.release(j, tc)
                state["b" + n + "_in"], state["b" + n] = tc, []
            yield 0.5

        def prep_mod(L):
            for half in range(2):
                i, bank, bw = work.take()
                for k in range(8):
                    j, raw, rw = wr.take()
                    tr = load(f"l_w{j}", raw[:], A[f"We{L}"][k * 128:(k + 1) * 128, half * 512:(half + 1) * 512], rw)
                    tm = put("pe", lambda e, k=k, r=raw, b_=bank: e.matmul(
                        b_[0:B, :], cS[:, k, :], r[:], start=(k == 0), stop=(k == 7)), [tr, t_cS, bw], "e_mm")
                    wr.release(j, tm)
                    yield 0.5
                j, raw, rw = wr.take()
                tb_ = load(f"l_w{j}", raw[0:B, :], A[f"be{L}"][half * 512:(half + 1) * 512].partition_broadcast(B), rw)
                ta = put("dve", lambda e, r=raw, b_=bank: e.tensor_tensor(r[0:B, :], b_[0:B, :], r[0:B, :], ALU.add),
                         [tb_, tm], "e_row")
                work.release(i, ta)
                i, bank, bw = work.take()
                for c in range(NC):
                    tt = put("pe", lambda e, c=c, r=raw, b_=bank: e.transpose(
                        b_[:, c * B:(c + 1) * B], r[0:B, c * 128:(c + 1) * 128], ident[0:B, 0:B]),
                        [ta, t_id, bw], "e_tr")
                wr.release(j, tt)
                src = bank[:, 0:NC * B].rearrange("p (c b) -> p c b", c=NC)
                if half == 0:
                    t1 = put("dve", lambda e, s=src: e.tensor_scalar(mod[:, 0], s, 1.0, 0.5, ALU.add, ALU.mult),
                             [tt, state["mod"]], "e_mod")
                    work.release(i, t1)
                else:
                    for c in range(NC):
                        t2 = put("dve", lambda e, c=c, s=src: e.tensor_scalar(
                            mod[:, 1, c, :], s[:, c, :], 0.5, None, ALU.mult), [tt, state["mod"]], "e_mod")
                    work.release(i, t2)
                    for c in range(NC):
                        t3 = put("dve", lambda e, c=c: e.scalar_tensor_tensor(
                            out=mod[:, 1, c, :], in0=mod[:, 0, c, :], scalar=cols[:, 12 + c:13 + c],
                            in1=mod[:, 1, c, :], op0=ALU.mult, op1=ALU.add), [t1, t2, state["cols_in"]], "e_mod")
                    for c in range(NC):
                        t3 = put("dve", lambda e, c=c: e.tensor_scalar(
                            mod[:, 0, c, :], mod[:, 0, c, :], cols[:, 8 + c:9 + c], None, ALU.mult),
                            [t3, state["cols_in"]], "e_mod")
                    state["mod_in"], state["mod"] = t3, []
                    state["cols"] += [t3]
                yield 0.5

        lnpar = [0]
        lnfree = {0: [], 1: []}

        def norm(src, dst, tin, tfree, nm_):
            p = lnpar[0] % 2
            lnpar[0] += 1
            for t in range(NT):
                ta = put("dve", lambda e, t=t: e.bn_stats(st[:, p, t, :], src[:, t, :]), [tin[t]], "ln_st")
            for t in range(NT):
                tg = put("dve", lambda e, t=t: e.bn_aggr(mv[:, p, t, :], st[:, p, t, :]),
                         [(ta[0], ta[1] - NT + 1 + t), lnfree[p]], "ln_mv")
            tv = put("dve", lambda e: e.tensor_scalar(ve[:, p, :], mv[:, p, :, 1], EPS, None, ALU.add), [tg], "ln_ve")
            tr = put("pool", lambda e: e.tensor_tensor(rs[:, p, :], ve[:, p, :], mhalf[:], ALU.pow), [tv, t_mh], "ln_rs")
            tn = put("dve", lambda e: e.scalar_tensor_tensor(out=nm[:, p, :], in0=mv[:, p, :, 0], scalar=-1.0,
                                                             in1=rs[:, p, :], op0=ALU.mult, op1=ALU.mult),
                     [tr, tg], "ln_nm")
            res = []
            for t in range(NT):
                res.append(put("pool", lambda e, t=t: e.tensor_scalar(
                    dst[:, t, :], src[:, t, :], rs[:, p, t:t + 1], nm[:, p, t:t + 1], ALU.mult, ALU.add),
                    [tn, tr, tfree], nm_))
            lnfree[p] = [res[-1]]
            return res

        def turn(bank, srcs, waits, name):
            for t, s in enumerate(srcs):
                r = put("pe", lambda e, t=t, s=s: e.transpose(bank[:, t * 128:(t + 1) * 128], s, ident[:]),
                        [waits, t_id], name)
            return r

        def product(bank, lh, ll, rh, rl, waits, name, kw=None):
            for k in range(NC):
                def f(e, k=k):
                    e.matmul(bank[:], lh(k), rh(k), start=(k == 0), stop=False)
                    e.matmul(bank[:], lh(k), rl(k), start=False, stop=False)
                    return e.matmul(bank[:], ll(k), rh(k), start=False, stop=(k == NC - 1))
                r = put("pe", f, [waits, kw[k]] if kw else waits, name)
                yield r

        xs = {"free": [], "T": None}

        def xbuf(L, b):
            return xin if L == 0 or b % 2 == 0 else vf

        def load_x(L, b, waits):
            src = A["x"] if L == 0 else x1d
            xs["in", L, b] = load(f"l_x{b % 2}", xbuf(L, b)[:],
                                  src[b].rearrange("(t p) d -> p t d", p=128), waits)

        def norm_x(L, b):
            buf = xbuf(L, b)
            xs["n", L, b] = norm(buf, buf, [xs["in", L, b]] * NT, [], "xn")

        def turn_x(L, b):
            buf = xbuf(L, b)
            xt = []
            for c in range(NC):
                i, bank, bw = work.take()
                tt = turn(bank, [buf[:, t, c * 128:(c + 1) * 128] for t in range(NT)], [xs["n", L, b], bw], "xn_tr")
                th = put("act", lambda e, c=c, b_=bank: e.copy(xTh[:, c, :], b_[:]), [tt, xs["free"]], "xT_hi")
                tl = put("dve", lambda e, c=c, b_=bank: e.tensor_tensor(
                    xTl[:, c, :], b_[:], xTh[:, c, :].bitcast(F32), ALU.subtract), [tt, th, xs["free"]], "xT_lo")
                work.release(i, th, tl)
                xt.append([th, tl])
                yield 0.8
            xs["turned", L, b] = [tt]
            xs["T"] = xt
            if L == 0 and b + 1 < B:
                load_x(0, b + 1, [tt])

        def channel_major(n, g):
            return (lambda k: Wh[n][:, k, g * 128:(g + 1) * 128], lambda k: Wl[n][:, k, g * 128:(g + 1) * 128],
                    lambda k: xTh[:, k, :], lambda k: xTl[:, k, :])

        def token_major(n, t):
            return (lambda k: xTh[:, k, t * 128:(t + 1) * 128], lambda k: xTl[:, k, t * 128:(t + 1) * 128],
                    lambda k: Wh[n][:, k, :], lambda k: Wl[n][:, k, :])

        ys = {}


        def norm_y(L, b, ty):
            ys["n"] = norm(yb, yb, ty, [], "yn")

        def silu_y(L, b):
            bk = aux2 if L == 0 else work
            ys["T"] = []
            for c in range(NC):
                i, bank, bw = bk.take()
                tt = turn(bank, [yb[:, t, c * 128:(c + 1) * 128] for t in range(NT)], [ys["n"], bw], "yn_tr")
                ta = put("act", lambda e, c=c, b_=bank: e.activation(
                    tb[:], b_[:], ACT.Tanh, scale=mod[:, 0, c, b:b + 1], bias=mod[:, 1, c, b:b + 1]),
                    [tt, state["mod_in"], yfree["t"]], "y_tanh")
                tu = put("dve", lambda e, c=c, b_=bank: e.tensor_scalar(
                    ub[:], b_[:], mod[:, 0, c, b:b + 1], mod[:, 1, c, b:b + 1], ALU.mult, ALU.add),
                    [tt, ta, state["mod_in"], yfree["s"]], "y_u")
                bk.release(i, ta, tu)
                tsf = put("dve", lambda e: e.scalar_tensor_tensor(out=ub[:], in0=tb[:], scalar=1.0, in1=ub[:],
                                                                 op0=ALU.add, op1=ALU.mult), [ta, tu], "y_s")
                yfree["t"] = [tsf]
                tsh = put("pool", lambda e, c=c: e.tensor_scalar(sTh[:, c, :], ub[:], 1.0, 0.0, ALU.mult, ALU.add),
                          [tsf, yfree["sT"]], "s_hi")
                tsl = put("pool", lambda e, c=c: e.tensor_tensor(sTl[:, c, :], ub[:], sTh[:, c, :].bitcast(F32),
                                                                 ALU.subtract), [tsf, tsh, yfree["sT"]], "s_lo")
                yfree["s"] = [tsl]
                ys["T"].append([tsh, tsl])
                yield 0.8
            yfree["yb"] = [tt]
            state["mod"] = [ta, tu]

        def out_y(L, b, tiles):
            bk = aux2 if L == 0 else work
            xsrc = A["x"] if L == 0 else x1d
            for t in tiles:
                j, xt, xw = wr.take()
                tx = load(f"l_w{j}", xt[:], xsrc[b, t * 128:(t + 1) * 128, :], xw)
                tx = put("pool", lambda e, x=xt: e.tensor_tensor(x[:], x[:], boB[:], ALU.add),
                         [tx, state["bo_in"]], "xb")
                i, bank, bw = bk.take()
                for tm in product(bank, lambda k, t=t: sTh[:, k, t * 128:(t + 1) * 128],
                                  lambda k, t=t: sTl[:, k, t * 128:(t + 1) * 128],
                                  lambda k: Wh["o"][:, k, :], lambda k: Wl["o"][:, k, :],
                                  [state["w"]["o"], bw], "o_mm", ys["T"]):
                    yield 0.65
                to = put("dve", lambda e, x=xt, b_=bank: e.tensor_tensor(x[:], b_[:], x[:], ALU.add), [tm, tx], "o_add")
                bk.release(i, to)
                dst = x1d if L == 0 else out
                tst = load(f"st{j}", dst[b, t * 128:(t + 1) * 128, :], xt[:], [to])
                wr.release(j, tst)
                stored.setdefault((L, b), []).append(tst)
            state["bo"] = [tx]
            yfree["sT"] = [tm]
            wfree["o"] = [tm]

        f0 = {"ET": [], "E": [], "v": [], "eq": [], "A": [], "qs": {0: [], 1: []}, "ks": {0: [], 1: []}}
        za = put("dve", lambda e: e.memset(Ah[:].bitcast(F32), 0.0), sig="a_set")
        zb = put("dve", lambda e: e.memset(Al[:].bitcast(F32), 0.0), sig="a_set")
        put("dve", lambda e: e.memset(Ah[0:64, :, 128:129].bitcast(F32), 1.0), [za], sig="a_set")
        t_as = put("dve", lambda e: e.memset(Ah[64:128, :, 129:130].bitcast(F32), 1.0), [za], sig="a_set")
        r0 = {}

        def k0(b):
            p = b % 2
            im, mrow_, mw = mB.take()
            tm_ = load("l_mB", mrow_[:], A["m0"][b].partition_broadcast(128), mw)
            tmb = put("dve", lambda e, m=mrow_: e.tensor_scalar(m[:], m[:], 1.0, NEG, ALU.subtract, ALU.mult), [tm_], "mB")
            for g in range(NC):
                i, bank, bw = work.take()
                for tm in product(bank, *channel_major("k", g), [state["w"]["k"], bw], "k_mm", xs["T"]):
                    yield 0.65
                j, kb, kw = vt.take()
                tk = put("dve", lambda e, k=kb, b_=bank, m=mrow_, g=g: e.tensor_tensor_reduce(
                    k[:], b_[:], m[:], 1.0, -3.0e38, ALU.add, ALU.max, kmx[:, p, g:g + 1]),
                    [tm, tmb, kw, f0["ks"][p]], "k_max")
                work.release(i, tk)
                t1 = put("dve", lambda e, g=g: e.tensor_tensor(kmb[:, p, g:g + 1], kmx[:, p, g:g + 1],
                                                               bkc[:, g:g + 1], ALU.add), [tk, state["bk_in"]], "k_mb")
                t1 = put("dve", lambda e, g=g: e.tensor_tensor(knb[:, p, g:g + 1], bkc[:, g:g + 1],
                                                               kmb[:, p, g:g + 1], ALU.subtract), [t1], "k_mb")
                te = put("act", lambda e, k=kb, g=g: e.activation(ET[:, g, :], k[:], ACT.Exp,
                                                                  bias=knb[:, p, g:g + 1],
                                                                  accum_out=ksm[:, p, g:g + 1]),
                         [tk, t1, f0["ET"], f0["ks"][p]], "k_exp")
                vt.release(j, te)
            mB.release(im, tk)
            wfree["k"] = [tm]
            state["bk"] = [t1]
            r0["ET", b] = [te]
            r0["krc", b] = put("dve", lambda e: e.reciprocal(krc[:, p, :], ksm[:, p, :]), [te, f0["ks"][p]], "k_rc")

        def v0(b):
            for t in range(NT):
                i, bank, bw = work.take()
                for tm in product(bank, *token_major("v", t), [state["w"]["v"], bw], "v_mm", xs["T"]):
                    yield 0.65
                j, vb, vw = vt.take()
                ta = put("dve", lambda e, v=vb, b_=bank: e.tensor_tensor(v[:], b_[:], bvB[:], ALU.add),
                         [tm, state["bv_in"], vw], "v_add")
                work.release(i, ta)
                th = put("act", lambda e, v=vb, t=t: e.activation(vh[:, t, :], v[:], ACT.Identity,
                                                                  scale=mk[:, b, t:t + 1]), [ta, t_mk, f0["v"]], "v_hi")
                tl = put("dve", lambda e, v=vb, t=t: e.scalar_tensor_tensor(
                    out=vl[:, t, :], in0=v[:], scalar=mk[:, b, t:t + 1], in1=vh[:, t, :].bitcast(F32),
                    op0=ALU.mult, op1=ALU.subtract), [ta, th, f0["v"]], "v_lo")
                vt.release(j, th, tl)
            wfree["v"] = [tm]
            state["bv"] = [ta]
            r0["v", b] = [th, tl]

        def q0(b):
            for t in range(NT):
                i, bank, bw = work.take()
                for tm in product(bank, *token_major("q", t), [state["w"]["q"], bw], "q_mm", xs["T"]):
                    yield 0.65
                j, qb, qw = vt.take()
                ta = put("dve", lambda e, v=qb, b_=bank: e.tensor_tensor(v[:], b_[:], bqB[:], ALU.add),
                         [tm, state["bq_in"], qw], "q_add")
                work.release(i, ta)
                v3 = qb[:].rearrange("p (h d) -> p h d", h=H0)
                tx = put("dve", lambda e, v=v3, t=t: e.tensor_reduce(qmx[:, t % 2, :], v, AX.X, ALU.max),
                         [ta, f0["qs"][t % 2]], "q_max")
                tsb = put("pool", lambda e, v=v3, t=t: e.tensor_tensor(
                    v, v, qmx[:, t % 2, :].unsqueeze(2).to_broadcast([128, H0, 64]), ALU.subtract), [tx], "q_sub")
                f0["qs"][t % 2] = [tsb]
                te = put("act", lambda e, v=qb, t=t: e.activation(eq[:, t, :], v[:], ACT.Exp), [tsb, f0["eq"]], "q_exp")
                vt.release(j, te)
            wfree["q"] = [tm]
            state["bq"] = [ta]
            xs["free"] = [tm]
            r0["eq", b] = [te]

        def turn_e0(b):
            for t in range(NT):
                i, bank, bw = aux.take()
                tt = turn(bank, [ET[:, g, t * 128:(t + 1) * 128] for g in range(NC)], [r0["ET", b], bw], "E_tr")
                th = put("act", lambda e, t=t, b_=bank: e.copy(Eh[:, t, :], b_[:]), [tt, f0["E"]], "E_hi")
                tl = put("dve", lambda e, t=t, b_=bank: e.tensor_tensor(
                    El[:, t, :], b_[:], Eh[:, t, :].bitcast(F32), ALU.subtract), [tt, th, f0["E"]], "E_lo")
                aux.release(i, th, tl)
                yield 0.8
            f0["ET"] = [tt]
            r0["E", b] = [th, tl]

        def state0(b):
            p = b % 2
            i, bank, bw = aux.take()
            for g in range(NC):
                def f(e, g=g, b_=bank):
                    n = slice(g * 128, (g + 1) * 128)
                    for t in range(NT):
                        e.matmul(b_[:, n], Eh[:, t, n], vh[:, t, n], start=(t == 0), stop=False)
                        e.matmul(b_[:, n], Eh[:, t, n], vl[:, t, n], start=False, stop=False)
                        r = e.matmul(b_[:, n], El[:, t, n], vh[:, t, n], start=False, stop=(t == NT - 1))
                    return r
                ta = put("pe", f, [r0["E", b], r0["v", b], bw], "att")
                yield 0.65
            f0["E"], f0["v"] = [ta], [ta]
            b3 = bank[:].rearrange("p (g n) -> p g n", g=NC)
            tz = []
            for h in range(2):
                r_ = slice(64 * h, 64 * h + 64)
                tf = put("dve", lambda e, r_=r_, h=h, b3=b3: e.tensor_tensor(
                    Af[r_], b3[r_, :, 64 * h:64 * h + 64],
                    krc[r_, p, :].unsqueeze(2).to_broadcast([64, NC, 64]), ALU.mult),
                    [ta, r0["krc", b], f0["A"]], "A_sc")
                tz.append(tf)
                th2 = put("act", lambda e, r_=r_, h=h: e.copy(Ah[r_, :, 64 * h:64 * h + 64], Af[r_]),
                          [tf, f0["A"], t_as], "A_hi")
                tl2 = put("dve", lambda e, r_=r_, h=h: e.tensor_tensor(
                    Al[r_, :, 64 * h:64 * h + 64], Af[r_], Ah[r_, :, 64 * h:64 * h + 64].bitcast(F32), ALU.subtract),
                    [tf, th2, f0["A"]], "A_lo")
            aux.release(i, *tz)
            f0["ks"][p] = [tz[-1]]
            r0["A", b] = [th2, tl2]
            f0["Aw"] = [tl2]

        def y0(b):
            held = None
            for g in range(NC + 1):
                nxt = None
                if g < NC:
                    i, bank, bw = aux.take()
                    tt = turn(bank, [eq[:, t, g * 128:(g + 1) * 128] for t in range(NT)], [r0["eq", b], bw], "q_tr")
                    jh, ah, wh_ = qh.take()
                    jl, al, wl_ = ql.take()
                    th = put("act", lambda e, a=ah, b_=bank: e.copy(a[:], b_[:]), [tt, wh_], "qT_hi")
                    tl = put("dve", lambda e, a=al, h=ah, b_=bank: e.tensor_tensor(
                        a[:], b_[:], h[:].bitcast(F32), ALU.subtract), [tt, th, wl_], "qT_lo")
                    aux.release(i, th, tl)
                    nxt = (g, jh, ah, jl, al, th, tl)
                    yield 0.8
                if held is not None:
                    hg, jh, ah, jl, al, th, tl = held
                    for half in range(2):
                        i, bank, bw = aux2.take()

                        def f(e, half=half, g=hg, b_=bank, ah=ah, al=al):
                            for u in range(2):
                                t = 2 * half + u
                                n, o = slice(t * 128, (t + 1) * 128), b_[:, u * 130:(u + 1) * 130]
                                e.matmul(o, ah[:, n], Ah[:, g, :], start=True, stop=False)
                                e.matmul(o, ah[:, n], Al[:, g, :], start=False, stop=False)
                                r = e.matmul(o, al[:, n], Ah[:, g, :], start=False, stop=True)
                            return r
                        tm = put("pe", f, [th, tl, r0["A", b], bw], "y_mm")
                        y3 = bank[:, 0:260].rearrange("p (u n) -> p u n", u=2)
                        tr = put("dve", lambda e, y3=y3: e.reciprocal(
                            yrc[:].rearrange("p (u h) -> p u h", u=2), y3[:, :, 128:130]),
                            [tm, f0.get("yrc", [])], "y_rc")
                        o4 = yb[:, 2 * half:2 * half + 2, hg * 128:(hg + 1) * 128]
                        ty = put("dve", lambda e, o4=o4, y3=y3: e.tensor_tensor(
                            o4.rearrange("p u (h d) -> p u h d", h=2),
                            y3[:, :, 0:128].rearrange("p u (h d) -> p u h d", h=2),
                            yrc[:].rearrange("p (u h) -> p u h", u=2).unsqueeze(3).to_broadcast([128, 2, 2, 64]),
                            ALU.mult), [tr, yfree["yb"]], "y_sc")
                        aux2.release(i, ty)
                        f0["yrc"] = [ty]
                        yield 0.45
                    qh.release(jh, tm)
                    ql.release(jl, tm)
                held = nxt
            f0["eq"] = [tt]
            f0["A"] = [tm]
            r0["y", b] = [ty] * NT

        s1 = {"stack": {0: [], 1: []}, "qsg": [], "ksg": [], "v": [], "Ps": [], "yT": [], "dT": [], "nx": {0: [], 1: []},
              "mr": [], "rd": [], "nxd": [], "pv": [], "den": []}
        r1 = {}
        mf = {}

        def begin1(after):
            mrow, mrh, mrl = yT[0:B, :], sg["q"][0:B, 0, :], sg["q"][0:B, 1, :]
            tm_ = load("l_mr", mrow, A["m1"], after)
            t1 = put("dve", lambda e: e.tensor_scalar(mrow, mrow, 1.0, NEG, ALU.subtract, ALU.mult), [tm_], "mr")
            t2 = put("act", lambda e: e.copy(mrh, mrow), [t1, after], "mr_hi")
            t3 = put("dve", lambda e: e.tensor_tensor(mrl, mrow, mrh.bitcast(F32), ALU.subtract),
                     [t1, t2, after], "mr_lo")
            mf["m"] = [load("l_mrs0", md[0], mrh, [t2]), load("l_mrs1", md[1], mrl, [t3])]
            s1["qsg"], s1["yT"] = mf["m"], [t2, t3]
            for i in range(2):
                ta = put("dve", lambda e, i=i: e.memset(Qs[i][RM:RM + 32].bitcast(F32), 1.0), after, "st_set")
                tb_ = put("dve", lambda e, i=i: e.memset(Ks[i][RM:RM + 32].bitcast(F32), 1.0), after, "st_set")
                s1["stack"][i] = [ta, tb_]
            mf["after"] = after

        def v1(b, tiles=range(NT)):
            for t in tiles:
                i, bank, bw = work.take()
                for tm in product(bank, *token_major("v", t), [state["w"]["v"], bw], "v_mm", xs["T"]):
                    yield 0.65
                j, vb, vw = vt.take()
                ta = put("dve", lambda e, v=vb, b_=bank: e.tensor_tensor(v[:], b_[:], bvB[:], ALU.add),
                         [tm, state["bv_in"], vw], "v_add")
                work.release(i, ta)
                tv = put("pool", lambda e, v=vb, t=t: e.tensor_scalar(
                    xbuf(1, b)[:, t, :], v[:], mk[:, b, t:t + 1], 1.0, ALU.mult, ALU.mult),
                    [ta, t_mk1, xs["turned", 1, b], mf["after"]], "v_out")
                vt.release(j, tv)
            wfree["v"] = [tm]
            r1["v", b] = [tv]

        def qk1(b, g):
            par = (4 * b + g) % 2
            for n in "qk":
                col = bqc if n == "q" else bkc
                i, bank, bw = work.take()
                for tm in product(bank, *channel_major(n, g), [state["w"][n], bw], n + "_mm", xs["T"]):
                    yield 0.65
                hi, lo = sg[n][:, 0, :], sg[n][:, 1, :]
                th = put("act", lambda e, a=hi, b_=bank, c=col: e.activation(
                    a, b_[:], ACT.Identity, bias=c[:, g:g + 1]),
                    [tm, s1[n + "sg"], mf["after"], state["b" + n + "_in"]], n + "_hi")
                tl = put("dve", lambda e, a=lo, h=hi, b_=bank, c=col: e.scalar_tensor_tensor(
                    out=a, in0=b_[:], scalar=c[:, g:g + 1], in1=h.bitcast(F32),
                    op0=ALU.add, op1=ALU.subtract), [tm, th, s1[n + "sg"], mf["after"]], n + "_lo")
                work.release(i, th, tl)
                ts = load(f"stq_{n}{par}", qkd[par, "qk".index(n)].rearrange("s p n -> p s n"), sg[n][:],
                          [th, tl, r1.get(("ld", n, par))])
                s1[n + "sg"] = [ts]
                r1[n, b, g] = ts
            if g == NG - 1:
                xs["free"] = [tm]

        def stack1(b, g):
            par = (4 * b + g) % 2
            free = [s1["stack"][par], mf["after"]]
            r1["stack", b, g] = []
            for n, S, rows in (("q", Qs[par], (0, 0, 1)), ("k", Ks[par], (0, 1, 0))):
                for r, p in enumerate(rows):
                    td = load(f"stk{n}{par}", S[32 * r:32 * r + 32, :, :],
                              qkd[par, "qk".index(n), p].rearrange("(j r) n -> r j n", r=32),
                              [r1[n, b, g], free])
                r1["ld", n, par] = [td]
                r1["stack", b, g].append(td)
            if g < 2:
                td = load(f"stm{par}", Ks[par][RM:RM + 2, :, :],
                          md[:, b, :].unsqueeze(1).to_broadcast([2, 4, T]), [mf["m"], free])
                r1["stack", b, g].append(td)

        def max1(b, g):
            par = (4 * b + g) % 2
            for j in range(4):
                for t in range(NT):
                    i, bank, bw = sbank.take()
                    tm = put("pe", lambda e, j=j, t=t, b_=bank: e.matmul(
                        b_[:], Qs[par][0:RX, j, t * 128:(t + 1) * 128], Ks[par][0:RX, j, :], start=True, stop=True),
                        [r1["stack", b, g], bw], "S")
                    tx = put("dve", lambda e, j=j, t=t, b_=bank: e.tensor_reduce(
                        nx[:, par, j * NT + t:j * NT + t + 1], b_[:], AX.X, ALU.max, negate=True),
                        [tm, s1["nx"][par], mf["after"]], "S_max")
                    sbank.release(i, tx)
                    yield 0.216
            i, bank, bw = sbank.take()
            tt = put("pe", lambda e, b_=bank: e.transpose(b_[0:16, 0:128], nx[:, par, :], ident[:]), [tx, bw], "nx_tr")
            th = put("act", lambda e, b_=bank: e.copy(nxh[:], b_[0:16, 0:128]), [tt, s1["nxd"]], "nx_hi")
            tl = put("dve", lambda e, b_=bank: e.tensor_tensor(
                nxl[:], b_[0:16, 0:128], nxh[:].bitcast(F32), ALU.subtract),
                [tt, th, s1["nxd"]], "nx_lo")
            sbank.release(i, th, tl)
            s1["nx"][par] = [tt]
            for r, src in ((RX, nxh), (RX + 1, nxl)):
                td = load(f"nxd{par}", Qs[par][r:r + 1, :, :].rearrange("p j (t n) -> p (j t) n", t=NT),
                          src[:], [th, tl, tm])
            s1["nxd"] = [td]
            r1["nx", b, g] = [td]

        def att1(b, g, after_st):
            par = (4 * b + g) % 2
            prev = None

            def pv(m, pb, te):
                def f(e, m=m, pb=pb):
                    for j in range(4):
                        h = 4 * g + j
                        r = e.matmul(PV[32 * j:32 * j + 32, :], xbuf(1, b)[:, m, h * 32:(h + 1) * 32], pb[:, j, :],
                                     start=(m == 0), stop=(m == NT - 1))
                    return r
                return put("pe", f, [te, r1["v", b], s1["pv"]], "PV")

            tps = None
            for m in range(NT + 1):
                if m < NT:
                    ip, pb, pw = Pb.take()
                    te = []
                    for j in range(4):
                        i, bank, bw = tbank.take()
                        tm = put("pe", lambda e, j=j, m=m, b_=bank: e.matmul(
                            b_[:], Ks[par][0:RE, j, m * 128:(m + 1) * 128], Qs[par][0:RE, j, :], start=True, stop=True),
                            [r1["nx", b, g], bw], "ST")
                        te.append(put("act", lambda e, j=j, b_=bank, pb=pb: e.activation(
                            pb[:, j, :], b_[:], ACT.Exp), [tm, pw, mf["after"]], "P"))
                        tbank.release(i, te[-1])
                        yield 0.216
                    if m == NT - 1:
                        s1["stack"][par] = [tm]
                        if after_st is not None:
                            after_st()
                if prev is not None:
                    pm, pip, ppb, pte = prev
                    tpv = pv(pm, ppb, pte)
                    yield 1.1
                    if pm == 0:
                        ik, pk, tk = pip, ppb, tpv
                    else:
                        eng = "dve" if pm == 1 else "pool"
                        for j in range(4):
                            tps = put(eng, lambda e, j=j, a=pk, c=ppb: e.tensor_tensor(
                                a[:, j, :], a[:, j, :], c[:, j, :], ALU.add), [pte, tk, tps], f"Ps_{eng}")
                        Pb.release(pip, tpv, tps)
                if m < NT:
                    prev = (m, ip, pb, te)
            tcy = put("act", lambda e: e.copy(yT[:], PV[:]), [tpv, s1["yT"], mf["after"]], "yT")
            if g == NG - 1 and b + 2 < B:
                load_x(1, b + 2, [tpv, stored[0, b + 2]])
            r1["tail", b, g] = (tcy, tps, ik, pk)

        def tail1(b, g):
            tcy, tps, ik, pk = r1["tail", b, g]
            ta = turn(PV, [yT[:, t * 128:(t + 1) * 128] for t in range(NT)], [tcy], "y1_tr")
            s1["yT"] = [ta]
            ty = put("act", lambda e: e.copy(yb[:, :, g * 128:(g + 1) * 128],
                                             PV[:].rearrange("p (t n) -> p t n", t=NT)), [ta, yfree["yb"]], "y1")
            s1["pv"] = [ty]
            yield 1.2

            def f(e):
                for j in range(4):
                    r = e.matmul(DEN[32 * j:32 * j + 32, :], sel[:, 4 - g:36 - g], pk[:, j, :],
                                 start=(g == 0), stop=(g == NG - 1))
                return r
            td = put("pe", f, [tps, s1["den"], t_sel], "den")
            Pb.release(ik, td)
            yield 1.1
            if g == NG - 1:
                tcd = put("act", lambda e: e.copy(dT[:], DEN[:]), [td, s1["dT"], mf["after"]], "dT")
                yield 1.0
                tb_ = turn(DEN, [dT[:, t * 128:(t + 1) * 128] for t in range(NT)], [tcd], "d1_tr")
                s1["dT"] = [tb_]
                tr = put("dve", lambda e: e.reciprocal(
                    rd[:].rearrange("p t g j -> p t j g"),
                    DEN[:].rearrange("p (t j l) -> p t j l", t=NT, j=4)[:, :, :, 0:4]),
                    [tb_, s1["rd"], mf["after"]], "rd")
                s1["den"] = [tr]
                ys_ = []
                for t in range(NT):
                    ys_.append(put("dve", lambda e, t=t: e.tensor_tensor(
                        yb[:, t, :].rearrange("p (h l) -> p h l", h=H1),
                        yb[:, t, :].rearrange("p (h l) -> p h l", h=H1),
                        rd[:, t, :, :].rearrange("p g j -> p (g j)").unsqueeze(2).to_broadcast([128, H1, 32]),
                        ALU.mult), [ty, tr], "y1_sc"))
                s1["rd"] = [ys_[-1]]
                norm_y(1, b, ys_)
                yield 0.8

        def run(*gs):
            for _ in chain(*gs):
                pass

        load_x(0, 0, [])
        norm_x(0, 0)
        run(prep_cols(0), prep_w(0, "k"), turn_x(0, 0))
        for b in range(B + 1):
            more, past, first = b < B, b >= 1, b == 0
            interleave((k0(b) if more else None, 10.4, 0, 1), (y0(b - 1) if past else None, 6.8, 0.05, 1))
            if past:
                norm_y(0, b - 1, r0["y", b - 1])
            interleave((chain(prep_w(0, "v") if first else None, v0(b) if more else None), 10.4, 0, 1),
                       (turn_e0(b) if more else None, 3.2, 0.3, 1))
            if b + 1 < B:
                norm_x(0, b + 1)
            interleave((chain(prep_w(0, "q") if first else None, q0(b) if more else None,
                              chain(prep_w(0, "o"), prep_mod(0)) if first else None), 10.4, 0, 1),
                       (state0(b) if more else None, 2.6, 0.2, 1),
                       (silu_y(0, b - 1) if past else None, 3.2, 0, 0.9))
            interleave((out_y(0, b - 1, range(NT)) if past else None, 10.4, 0, 1),
                       (turn_x(0, b + 1) if b + 1 < B else None, 3.2, 0, 0.9))
        after = list(flat([f0["A"], f0["E"], f0["v"], f0["eq"], f0["ET"], f0["yrc"], f0["ks"][0], f0["ks"][1],
                           r0["krc", B - 1], f0["Aw"], state["bq"], state["bk"]]))

        t_mk1 = load("l_mk1", mk[:], A["mk1"], [f0["v"]])
        t_sel = put("pool", lambda e: e.memset(sel[:], 0.0), after, "sel")
        t_sel = put("pool", lambda e: e.memset(sel[:, 4:5], 1.0), [t_sel], "sel")
        load_x(1, 0, [stored[0, 0], xs["turned", 0, B - 1]])
        load_x(1, 1, [stored[0, 1], after])
        norm_x(1, 0)
        begin1(after)
        run(prep_cols(1), prep_w(1, "q"), prep_w(1, "k"), turn_x(1, 0), qk1(0, 0))
        last_psum = [w for r in (aux, aux2) for _, w in r.free]
        for r in (sbank, tbank):
            r.free = [(i, last_psum) for i in range(2)]
        s1["pv"], s1["den"] = list(last_psum), list(last_psum)
        stack1(0, 0)
        run(prep_w(1, "v"), v1(0), qk1(0, 1))
        stack1(0, 1)
        interleave((max1(0, 0), 3.5, 0, 1), (chain(prep_w(1, "o"), prep_mod(1)), 20.0, 0, 1))
        seq = [(b, g) for b in range(B) for g in range(NG)]
        for n, (b, g) in enumerate(seq):
            nx1 = seq[n + 1] if n + 1 < len(seq) else None
            nx2 = seq[n + 2] if n + 2 < len(seq) else None
            fill, cost = [], 0.1
            if nx2:
                fill.append(qk1(*nx2))
                cost += 5.2
            if g == 0 and b >= 1:
                fill += [silu_y(1, b - 1), out_y(1, b - 1, range(0, 1))]
                cost += 5.8
            if g == 1 and b + 1 < B:
                fill += [turn_x(1, b + 1)]
                cost += 3.2
            if g in (1, 2) and b >= 1:
                fill += [out_y(1, b - 1, range(1, 2) if g == 1 else range(2, NT))]
                cost += 2.6 * g
            if g in (2, 3) and b + 1 < B:
                fill += [v1(b + 1, range(0, 1) if g == 2 else range(1, NT))]
                cost += 2.6 if g == 2 else 7.8
            if g == 0 and b + 1 < B:
                norm_x(1, b + 1)
            interleave((att1(b, g, (lambda: stack1(*nx2)) if nx2 else None), 7.8, 0.03, 1),
                       (tail1(*seq[n - 1]) if n else None, 2.3 if seq[n - 1][1] < NG - 1 else 4.1, 0, 0.3),
                       (max1(*nx1) if nx1 else None, 3.5, 0.1, 0.7),
                       (chain(*fill) if fill else None, cost, 0, 1 if len(fill) > 1 else 0.7))
        run(tail1(B - 1, NG - 1), silu_y(1, B - 1), out_y(1, B - 1, range(NT)))
        for j in range(2):
            c = Q.sem(f"st{j}")
            Q.q["sp"].append((lambda e: None, [(c, c.n)], None, 16))
        block = ctx.enter_context(nc.Block())

        @block.sync
        def _(e):
            Q.run("sp", e)

        @block.gpsimd
        def _(e):
            Q.run("pool", e)

        @block.scalar
        def _(e):
            Q.run("act", e)

        @block.vector
        def _(e):
            Q.run("dve", e)

        @block.tensor
        def _(e):
            Q.run("pe", e)


def kernel(**inputs):
    import numpy as np
    import concourse.bacc as bacc
    from concourse import mybir as mb
    from concourse.bass_utils import run_bass_kernel_spmd

    g = {k: np.asarray(v) for k, v in inputs.items()}

    def col(v):
        return v.reshape(NC, 128).T

    def mcol(m):
        return np.ascontiguousarray(m.reshape(B, NT, 128).transpose(2, 0, 1))

    P0, P1 = "L0_cond_", "L1_cond_"
    a = {
        "x": g["x"],
        "m0": g["mask_BxSx1_fk1"].reshape(B, T),
        "m1": g["mask_BxS_ff1"],
        "mk": mcol(g["mask_BxSx1_fk1"]),
        "mk1": mcol(g["mask_BxS_ff1"]),
        "cT": np.ascontiguousarray(g["cond_2048"].T.reshape(8, 128, B).transpose(1, 0, 2)),
        "cols0": np.concatenate([col(g[P0 + n]) for n in ("ln_w", "ln_b", "ln2_w", "ln2_b")], axis=1),
        "cols1": np.concatenate([col(g[P1 + n]) for n in ("norm_w", "norm_b", "sb_norm_w", "sb_norm_b")], axis=1),
        "Wq0": g[P0 + "Wq"], "bq0": g[P0 + "bq"], "Wk0": g[P0 + "Wk"], "bk0": g[P0 + "bk"],
        "Wv0": g[P0 + "Wv"], "bv0": g[P0 + "bv"], "We0": g[P0 + "W_emb"], "be0": g[P0 + "b_emb"],
        "Wo0": g[P0 + "W_out"], "bo0": g[P0 + "b_out"],
        "Wq1": g[P1 + "q_w"], "bq1": g[P1 + "q_b"], "Wk1": g[P1 + "k_w"], "bk1": g[P1 + "k_b"],
        "Wv1": g[P1 + "v_w"], "bv1": g[P1 + "v_b"], "We1": g[P1 + "emb_w"], "be1": g[P1 + "emb_b"],
        "Wo1": g[P1 + "out_w"], "bo1": g[P1 + "out_b"],
    }
    nc = bacc.Bacc("TRN2", target_bir_lowering=False, num_devices=1)
    arrays, aps = {}, {}
    for n, v in a.items():
        v = np.ascontiguousarray(v)
        arrays["in_" + n] = v
        aps[n] = nc.dram_tensor("in_" + n, v.shape, mb.dt.from_np(v.dtype), kind="ExternalInput").ap()
    out = nc.dram_tensor("out_0", (B, T, D), mb.dt.float32, kind="ExternalOutput").ap()
    cond_two_layers(nc, aps, out)
    r = run_bass_kernel_spmd(nc, [arrays], core_ids=[0])
    return r.results[0]["out_0"]
```

```python
from contextlib import ExitStack

import concourse.bass as bass
from concourse import mybir

ALU = mybir.AluOpType
ACT = mybir.ActivationFunctionType
AX = mybir.AxisListType
F32 = mybir.dt.float32
FR = mybir.dt.float32r

B, T, D, TE = 8, 512, 512, 1024
NT = T // 128
NC = D // 128
EPS = 1e-5
NEG = 1000000.0
H0, H1 = 8, 16
NG = 4
RM, RX, RE = 96, 98, 100
ADD = (("pool",) * 4, ("pool",) * 4, ("dve",) * 4)



class Counter:

    def __init__(self, handle):
        self.h, self.n = handle, 0

    def add(self, k):
        self.n += k
        return (self, self.n)


class Queues:

    def __init__(self, nc, ctx):
        self.nc, self.ctx, self.sems = nc, ctx, {}
        self.q = {e: [] for e in ("pe", "act", "dve", "pool", "sp")}
        self.seen = {e: {} for e in self.q}

    def sem(self, name):
        if name not in self.sems:
            self.sems[name] = Counter(self.ctx.enter_context(self.nc.semaphore("s_" + name)))
        return self.sems[name]

    def put(self, eng, fn, waits=(), sig=None):
        need = []
        for w in flat(waits):
            if self.seen[eng].get(w[0], 0) < w[1]:
                self.seen[eng][w[0]] = w[1]
                need.append(w)
        s = self.sem(sig) if sig else None
        step = 16 if eng == "sp" else 1
        self.q[eng].append((fn, need, s, step))
        return s.add(step) if s else None

    def run(self, eng, e):
        for fn, need, s, step in self.q[eng]:
            for c, v in need:
                e.wait_ge(c.h, v)
            ins = fn(e)
            if s:
                ins.then_inc(s.h, step)


def flat(ws):
    for w in ws:
        if w is None:
            continue
        if isinstance(w, tuple):
            yield w
        else:
            yield from flat(w)


def raw32(ap):
    return ap.bitcast(F32) if ap.dtype == FR else ap


class Ring:

    def __init__(self, bufs, name=""):
        self.bufs, self.name = bufs, name
        self.free = [(i, []) for i in range(len(bufs))]

    def take(self):
        assert self.free, "taken again before its readers were queued"
        i, w = self.free.pop(0)
        return i, self.bufs[i], w

    def release(self, i, *ticks):
        self.free.append((i, list(ticks)))


class Stream:

    def __init__(self, ring, load, items):
        self.ring, self.load, self.items, self.ready = ring, load, items, []
        self.fill()

    def fill(self):
        while self.items and self.ring.free:
            j, raw, w = self.ring.take()
            rows, src = self.items.pop(0)
            self.ready.append((j, raw, self.load(f"l_{self.ring.name}{j}", raw[0:rows, :], src, w)))

    def get(self):
        return self.ready.pop(0)

    def done(self, j, *ticks):
        self.ring.release(j, *ticks)
        self.fill()


def interleave(*gens):
    live = [[g, (b - a) / total, a] for g, total, a, b in gens if g is not None]
    while live:
        it = min(live, key=lambda x: x[2])
        try:
            it[2] += next(it[0]) * it[1]
        except StopIteration:
            live.remove(it)


def chain(*gens):
    for g in gens:
        if g is not None:
            yield from g


def cond_two_layers(nc, A, out):
    ctx = ExitStack()
    with ctx:
        Q = Queues(nc, ctx)
        put = Q.put

        def sb(name, shape, dt=F32, c=ctx):
            return c.enter_context(nc.sbuf_tensor(name, shape, dt))

        md = nc.dram_tensor("mask_scratch", [2, B, T], F32, kind="Internal").ap()
        qkd = nc.dram_tensor("stack_scratch", [2, 2, 2, 128, T], F32, kind="Internal").ap()
        x1d = nc.dram_tensor("x1_scratch", [B, T, D], F32, kind="Internal").ap()

        Wh = {n: sb("Wh_" + n, [128, NC, D], FR) for n in "qkvo"}
        Wl = {n: sb("Wl_" + n, [128, NC, D], FR) for n in "qkvo"}
        xin = sb("xin", [128, NT, D])
        xTh = sb("xTh", [128, NC, T], FR)
        xTl = sb("xTl", [128, NC, T], FR)
        yb = sb("yb", [128, NT, D])
        sTh = sb("sTh", [128, NC, T], FR)
        sTl = sb("sTl", [128, NC, T], FR)
        tbr = Ring([sb("tb0", [128, D]), sb("tb1", [128, D])])
        vt = Ring([sb("vt0", [128, D]), sb("vt1", [128, D])])
        wr = Ring([sb(f"wr{i}", [128, D]) for i in range(4)], "w")
        bvB = sb("bvB", [128, D])
        boB = sb("boB", [128, D])
        ident = sb("ident", [128, 128])
        ones = sb("ones", [128, 32])
        mhalf = sb("mhalf", [128, NT])
        cols = sb("cols", [128, 24])
        bqc = sb("bqc", [128, NC])
        bkc = sb("bkc", [128, NC])
        mk = sb("mk", [128, B, NT])
        mod = sb("mod", [128, 2, NC, B])
        cT = sb("cT", [128, 8, B])
        cS = sb("cS", [128, 8, B])
        cU = sb("cU", [128, 8, B])
        st = sb("st", [128, 2, NT, 6])
        mv = sb("mv", [128, 2, NT, 2])
        ve = sb("ve", [128, 2, NT])
        rs = sb("rs", [128, 2, NT])
        nm = sb("nm", [128, 2, NT])

        c0 = ExitStack()
        mB = Ring([sb("mB0", [128, T], c=c0)])
        ET = sb("ET", [128, NC, T], c=c0)
        Eh = sb("Eh", [128, NT, D], FR, c=c0)
        El = sb("El", [128, NT, D], FR, c=c0)
        vh = sb("vh", [128, NT, D], FR, c=c0)
        vl = sb("vl", [128, NT, D], FR, c=c0)
        eq = sb("eq", [128, NT, D], c=c0)
        qh = Ring([sb("qh0", [128, T], FR, c=c0), sb("qh1", [128, T], FR, c=c0)])
        ql = Ring([sb("ql0", [128, T], FR, c=c0), sb("ql1", [128, T], FR, c=c0)])
        bqB = sb("bqB", [128, D], c=c0)
        Af = sb("Af", [128, NC, 64], c=c0)
        Ah = sb("Ah", [128, NC, 130], FR, c=c0)
        Al = sb("Al", [128, NC, 130], FR, c=c0)
        qmx = sb("qmx", [128, 2, H0], c=c0)
        kmx = sb("kmx", [128, 2, NC], c=c0)
        kmb = sb("kmb", [128, 2, NC], c=c0)
        knb = sb("knb", [128, 2, NC], c=c0)
        ksm = sb("ksm", [128, 2, NC], c=c0)
        krc = sb("krc", [128, 2, NC], c=c0)
        yrc = sb("yrc", [128, 4], c=c0)
        c0.close()

        c1 = ctx
        Qs = [sb(f"Qs{i}", [128, 4, T], FR, c=c1) for i in range(2)]
        Ks = [sb(f"Ks{i}", [128, 4, T], FR, c=c1) for i in range(2)]
        sg = {n: sb("sg_" + n, [128, 2, T], FR, c=c1) for n in "qk"}
        vf = sb("vf", [128, NT, D], c=c1)
        Pb = Ring([sb(f"Pb{i}", [128, 4, T], c=c1) for i in range(3)])
        rd = sb("rd", [128, NT, NG, 4], c=c1)
        sel = sb("sel", [128, 36], c=c1)
        nx = sb("nx", [128, 2, 16], c=c1)
        nxh = sb("nxh", [16, 128], FR, c=c1)
        nxl = sb("nxl", [16, 128], FR, c=c1)

        ps = [ctx.enter_context(nc.psum_tensor(f"ps{i}", [128, 512], F32)) for i in range(8)]
        work = Ring(list(ps))
        PV, DEN = ps[6], ps[7]

        t_c = put("pool", lambda e: e.memset(ones[:], 1.0), sig="ones")
        t_c0 = put("pool", lambda e: e.memset(ident[:], 0.0), sig="const")
        t_id = put("pool", lambda e: e.affine_select(out=ident[:], in_=ident[:], compare_op=ALU.not_equal,
                                                     fill=1.0, base=0, pattern=[[-1, 128]],
                                                     channel_multiplier=1), [t_c0], sig="const")
        t_mh = put("pool", lambda e: e.memset(mhalf[:], -0.5), sig="const")

        def load(name, dst, src, waits=()):
            dst, src = raw32(dst), raw32(src)
            return put("sp", lambda e: e.dma_start(dst, src), waits, sig=name)

        t_mk = load("l_mk", mk[:], A["mk"])
        t_cT = load("l_cT", cT[:], A["cT"])

        t = put("act", lambda e: e.activation(cS[:], cT[:], ACT.Tanh, scale=0.5), [t_cT], "c_tanh")
        t2 = put("dve", lambda e: e.tensor_scalar(cU[:], cT[:], 0.5, None, ALU.mult), [t_cT], "c_half")
        t_cS = put("dve", lambda e: e.scalar_tensor_tensor(out=cS[:], in0=cS[:], scalar=1.0, in1=cU[:],
                                                           op0=ALU.add, op1=ALU.mult), [t, t2], "c_silu")

        state = {"set": [], "mod": [], "lnb": [], "cols": [], "bv": [], "bo": [], "bq": [], "bk": [], "w": {},
                 "lnb_use": [], "mod_scale": None}
        wfree = {n: [] for n in "qkvo"}
        yfree = {"yb": [], "sT": []}
        stored = {}

        def prep_cols(L):
            t = load(f"l_cols{L}", cols[:, 0:16], A[f"cols{L}"], [state["cols"]])
            i, lb, lw = vt.take()
            for c in range(NC):
                tl = put("dve", lambda e, c=c: e.tensor_scalar(lb[:, c * 128:(c + 1) * 128], ident[:], 0.0,
                                                               cols[:, 4 + c:5 + c], ALU.mult, ALU.add),
                         [t, t_id, lw], "lnb_b")
            state["cols_in"], state["lnb_in"] = t, tl
            state["lnb"] = [i, lb]
            state["cols"], state["lnb_use"] = [tl], []

        def prep_cols_end():
            vt.release(state["lnb"][0], *state["lnb_use"])

        def w_items(L, names):
            for n in names:
                for k in range(NC):
                    yield 128, A[f"W{n}{L}"][k * 128:(k + 1) * 128, :]
                if n == "k" or (n == "q" and L == 1):
                    yield 128, A[f"b{n}{L}"].partition_broadcast(128)

        def mod_items(L):
            for half in range(2):
                n = slice(half * 512, (half + 1) * 512)
                for k in range(8):
                    yield 128, A[f"We{L}"][k * 128:(k + 1) * 128, n]
                yield B, A[f"be{L}"][n].partition_broadcast(B)

        def prep_w(L, n, raws):
            bk = work
            fold = n != "o"
            i, bank, bw = bk.take() if fold else (None, None, [])
            row = bvB if n == "v" else bqB if n == "q" and L == 0 else boB if n == "o" else None
            if row is not None:
                trow = load(f"l_b{n}", row[:], A[f"b{n}{L}"].partition_broadcast(128), [state["b" + n]])
            for kt_ in range(NC):
                j, raw, tr = raws.get()
                sc = cols[:, kt_:kt_ + 1] if fold else 1.0
                hi, lo = Wh[n][:, kt_, :], Wl[n][:, kt_, :]
                th = put("act", lambda e, a=hi, r=raw, s=sc: e.activation(a, r[:], ACT.Identity, scale=s),
                         [tr, state["cols_in"], wfree[n]], f"w_hi")
                tl = put("dve", lambda e, a=lo, h=hi, r=raw, s=sc: e.scalar_tensor_tensor(
                    out=a, in0=r[:], scalar=s, in1=h.bitcast(F32), op0=ALU.mult, op1=ALU.subtract),
                    [tr, th, state["cols_in"], wfree[n]], "w_lo")
                if fold:
                    tm = put("pe", lambda e, k=kt_, r=raw, b_=bank, lb=state["lnb"][1]: e.matmul(
                        b_[:], lb[:, k * 128:(k + 1) * 128], r[:], start=(k == 0), stop=(k == NC - 1)),
                        [tr, state["lnb_in"], bw], "w_bias")
                    raws.done(j, th, tl, tm)
                else:
                    raws.done(j, th, tl)
                yield 1.0
            wfree[n] = []
            state["w"][n] = [th, tl]
            state["cols"] += [th, tl]
            if not fold:
                state["bo_in"], state["bo"] = trow, []
                return
            state["lnb_use"] += [tm]
            if row is not None:
                ta = put("dve", lambda e, d=row, b_=bank: e.tensor_tensor(d[:], b_[:], d[:], ALU.add),
                         [trow, tm], "b_row")
                bk.release(i, ta)
                state["b" + n + "_in"], state["b" + n] = ta, []
            else:
                col = bqc if n == "q" else bkc
                j, raw, tb_ = raws.get()
                ta = put("dve", lambda e, r=raw, b_=bank: e.tensor_tensor(r[:], b_[:], r[:], ALU.add),
                         [tb_, tm], "b_row")
                bk.release(i, ta)
                for c in range(NC):
                    td = put("dve", lambda e, r=raw, c=c: e.tensor_tensor(
                        r[:, c * 128:(c + 1) * 128], r[:, c * 128:(c + 1) * 128], ident[:], ALU.mult),
                        [ta, t_id], "b_diag")
                tc = put("dve", lambda e, r=raw, k=col: e.tensor_reduce(
                    k[:], r[:].rearrange("p (c n) -> p c n", c=NC), AX.X, ALU.add),
                    [td, state["b" + n]], "b_col")
                raws.done(j, tc)
                state["b" + n + "_in"], state["b" + n] = tc, []
            yield 1.0

        def prep_mod(L, raws, halves=range(2)):
            bk = work
            for half in halves:
                i, bank, bw = bk.take()
                for k in range(8):
                    j, raw, tr = raws.get()
                    tm = put("pe", lambda e, k=k, r=raw, b_=bank: e.matmul(
                        b_[0:B, :], cS[:, k, :], r[:], start=(k == 0), stop=(k == 7)), [tr, t_cS, bw], "e_mm")
                    raws.done(j, tm)
                    yield 0.9
                j, raw, tb_ = raws.get()
                ta = put("dve", lambda e, r=raw, b_=bank: e.tensor_tensor(r[0:B, :], b_[0:B, :], r[0:B, :], ALU.add),
                         [tb_, tm], "e_row")
                bk.release(i, ta)
                i, bank, bw = bk.take()
                for c in range(NC):
                    tt = put("pe", lambda e, c=c, r=raw, b_=bank: e.transpose(
                        b_[:, c * B:(c + 1) * B], r[0:B, c * 128:(c + 1) * 128], ident[0:B, 0:B]),
                        [ta, t_id, bw], "e_tr")
                raws.done(j, tt)
                src = bank[:, 0:NC * B].rearrange("p (c b) -> p c b", c=NC)
                if half == 0:
                    t1 = put("dve", lambda e, s=src: e.tensor_scalar(mod[:, 0], s, 1.0, 0.5, ALU.add, ALU.mult),
                             [tt, state["mod"]], "e_mod")
                    bk.release(i, t1)
                    state["mod_scale"] = t1
                else:
                    for c in range(NC):
                        t2 = put("dve", lambda e, c=c, s=src: e.tensor_scalar(
                            mod[:, 1, c, :], s[:, c, :], 0.5, None, ALU.mult), [tt, state["mod"]], "e_mod")
                    bk.release(i, t2)
                    for c in range(NC):
                        t3 = put("dve", lambda e, c=c: e.scalar_tensor_tensor(
                            out=mod[:, 1, c, :], in0=mod[:, 0, c, :], scalar=cols[:, 12 + c:13 + c],
                            in1=mod[:, 1, c, :], op0=ALU.mult, op1=ALU.add), [state["mod_scale"], t2, state["cols_in"]], "e_mod")
                    for c in range(NC):
                        t3 = put("dve", lambda e, c=c: e.tensor_scalar(
                            mod[:, 0, c, :], mod[:, 0, c, :], cols[:, 8 + c:9 + c], None, ALU.mult),
                            [t3, state["cols_in"]], "e_mod")
                    state["mod_in"], state["mod"] = t3, []
                    state["cols"] += [t3]
                yield 0.9

        lnpar = [0]
        lnfree = {0: [], 1: []}

        def norm(L, src, dst, tin, nm_, res, fast=False):
            p = lnpar[0] % 2
            lnpar[0] += 1
            for t in range(NT):
                ta = put("dve", lambda e, t=t: e.bn_stats(st[:, p, t, :], src[:, t, :]), [tin[t]], "ln_st")
                yield 0.4
                tg = put("dve", lambda e, t=t: e.bn_aggr(mv[:, p, t, :], st[:, p, t, :]), [ta, lnfree[p]], "ln_mv")
            tv = put("dve", lambda e: e.tensor_scalar(ve[:, p, :], mv[:, p, :, 1], EPS, None, ALU.add), [tg], "ln_ve")
            tn = put("dve", lambda e: e.tensor_scalar(nm[:, p, :], mv[:, p, :, 0], -1.0, None, ALU.mult), [tg], "ln_nm")
            tr = put("pool", lambda e: e.tensor_tensor(rs[:, p, :], ve[:, p, :], mhalf[:], ALU.pow), [tv, t_mh, state["set"]],
                     "ln_rs")
            tn = put("pool", lambda e: e.tensor_tensor(nm[:, p, :], nm[:, p, :], rs[:, p, :], ALU.mult), [tn, tr], "ln_nr")
            yield 0.2
            for t in range(NT):
                if L == 0 or (fast and t % 2):
                    res.append(put("pool", lambda e, t=t: e.tensor_scalar(
                        dst[:, t, :], src[:, t, :], rs[:, p, t:t + 1], nm[:, p, t:t + 1], ALU.mult, ALU.add),
                        [tn], nm_ + "p"))
                else:
                    res.append(put("act", lambda e, t=t: e.activation(
                        dst[:, t, :], src[:, t, :], ACT.Identity, scale=rs[:, p, t:t + 1], bias=nm[:, p, t:t + 1]),
                        [tn], nm_))
                yield 0.3
            lnfree[p] = res[-2:]

        def t4(x):
            return x[:, 0:512].rearrange("p (t n) -> p t n", t=NT)

        def turn(bank, srcs, waits, name):
            for t, s in enumerate(srcs):
                r = put("pe", lambda e, t=t, s=s: e.transpose(bank[:, t * 128:(t + 1) * 128], s, ident[:]),
                        [waits, t_id], name)
            return r

        def product(bank, lh, ll, rh, rl, waits, name, kw=None):
            for k in range(NC):
                def f(e, k=k):
                    e.matmul(bank[:], lh(k), rh(k), start=(k == 0), stop=False)
                    e.matmul(bank[:], lh(k), rl(k), start=False, stop=False)
                    return e.matmul(bank[:], ll(k), rh(k), start=False, stop=(k == NC - 1))
                r = put("pe", f, [waits, kw[k]] if kw else waits, name)
                yield r

        xs = {"free": [], "T": None}

        def xbuf(L, b):
            return xin if L == 0 or b % 2 == 0 else vf

        def load_x(L, b, waits):
            src = A["x"] if L == 0 else x1d
            xs["in", L, b] = load(f"l_x{b % 2}", xbuf(L, b)[:],
                                  src[b].rearrange("(t p) d -> p t d", p=128), waits)

        def norm_x(L, b):
            buf = xbuf(L, b)
            xs["n", L, b] = []
            yield from norm(L, buf, buf, [xs["in", L, b]] * NT, "xn", xs["n", L, b])

        def turn_x(L, b):
            buf = xbuf(L, b)
            xt = []
            bk = work
            for c in range(NC):
                i, bank, bw = bk.take()
                tt = turn(bank, [buf[:, t, c * 128:(c + 1) * 128] for t in range(NT)], [xs["n", L, b], bw], "xn_tr")
                th = put("act", lambda e, c=c, b_=bank: e.copy(xTh[:, c, :], b_[:]), [tt, xs["free"]], "xT_hi")
                yield 0.3
                tl = put("dve", lambda e, c=c, b_=bank: e.tensor_tensor(
                    xTl[:, c, :], b_[:], xTh[:, c, :].bitcast(F32), ALU.subtract), [tt, th, xs["free"]], "xT_lo")
                bk.release(i, th, tl)
                xt.append([th, tl])
                yield 0.5
            xs["turned", L, b] = [tt]
            xs["T"] = xt
            if L == 0 and b + 1 < B:
                load_x(0, b + 1, [tt])

        def channel_major(n, g):
            return (lambda k: Wh[n][:, k, g * 128:(g + 1) * 128], lambda k: Wl[n][:, k, g * 128:(g + 1) * 128],
                    lambda k: xTh[:, k, :], lambda k: xTl[:, k, :])

        def token_major(n, t):
            return (lambda k: xTh[:, k, t * 128:(t + 1) * 128], lambda k: xTl[:, k, t * 128:(t + 1) * 128],
                    lambda k: Wh[n][:, k, :], lambda k: Wl[n][:, k, :])

        ys = {}

        def norm_y(L, b, ty):
            ys["n"] = []
            yield from norm(L, yb, yb, ty, "yn", ys["n"], L == 1 and b == B - 1)

        def add_bo(t):
            j, xt, tx = ys["x", t]
            ys["x", t] = (j, xt, put("pool", lambda e: e.tensor_tensor(xt[:], xt[:], boB[:], ALU.add),
                                     [tx, state["bo_in"]], "xb"))

        def silu_y(L, b):
            bk = work
            ys["T"] = []
            xsrc = A["x"] if L == 0 else x1d
            for t in range(NT):
                j, xt, xw = wr.take()
                ys["x", t] = (j, xt, load(f"l_w{j}", xt[:], xsrc[b, t * 128:(t + 1) * 128, :], xw))
            tsf = None
            for c in range(NC + 1):
                if c < NC:
                    i, bank, bw = bk.take()
                    tt = turn(bank, [yb[:, t, c * 128:(c + 1) * 128] for t in range(NT)], [ys["n"], bw], "yn_tr")
                    j, th_, thw = tbr.take()
                    ta = put("act", lambda e, c=c, b_=bank, o=th_: e.activation(
                        o[:], b_[:], ACT.Tanh, scale=mod[:, 0, c, b:b + 1], bias=mod[:, 1, c, b:b + 1]),
                        [tt, state["mod_in"], thw], "y_tanh")
                    yield 0.3
                if c:
                    ov = yb[:, :, (c - 1) * 128:c * 128]
                    tsh = put("act", lambda e, c=c - 1, o=ov: e.copy(t4(sTh[:, c, :]), o), [tsf, yfree["sT"]], "s_hi")
                if c < NC:
                    yv = yb[:, :, c * 128:(c + 1) * 128]
                    tu = put("dve", lambda e, c=c, b_=bank, o=yv: e.tensor_scalar(
                        o, t4(b_), mod[:, 0, c, b:b + 1], mod[:, 1, c, b:b + 1], ALU.mult, ALU.add),
                        [tt, ta, state["mod_in"]], "y_u")
                    bk.release(i, ta, tu)
                    tsf_ = put("dve", lambda e, o=yv, h=th_: e.scalar_tensor_tensor(
                        out=o, in0=t4(h), scalar=1.0, in1=o, op0=ALU.add, op1=ALU.mult), [ta, tu], "y_s")
                    tbr.release(j, tsf_)
                if c:
                    tsl = put("dve" if L == 0 or b == B - 1 else "pool", lambda e, c=c - 1, o=ov: e.tensor_tensor(
                        t4(sTl[:, c, :]), o, t4(sTh[:, c, :].bitcast(F32)), ALU.subtract),
                        [tsf, tsh, yfree["sT"]], "s_lo")
                    ys["T"].append([tsh, tsl])
                    if L == 1:
                        add_bo(c - 1)
                tsf = tsf_
                yield 0.5
            yfree["yb"] = [tsh, tsl]
            state["mod"] = [ta, tu]

        def out_y(L, b, tiles):
            bk = work
            for t in tiles:
                if L == 0:
                    add_bo(t)
                j, xt, tx = ys["x", t]
                i, bank, bw = bk.take()
                for tm in product(bank, lambda k, t=t: sTh[:, k, t * 128:(t + 1) * 128],
                                  lambda k, t=t: sTl[:, k, t * 128:(t + 1) * 128],
                                  lambda k: Wh["o"][:, k, :], lambda k: Wl["o"][:, k, :],
                                  [state["w"]["o"], bw], "o_mm", ys["T"]):
                    yield 0.65
                to = put("dve", lambda e, x=xt, b_=bank: e.tensor_tensor(x[:], b_[:], x[:], ALU.add), [tm, tx], "o_add")
                bk.release(i, to)
                dst = x1d if L == 0 else out
                tst = load(f"st{j}", dst[b, t * 128:(t + 1) * 128, :], xt[:], [to])
                wr.release(j, tst)
                stored.setdefault((L, b), []).append(tst)
            state["bo"] = [tx]
            yfree["sT"] = [tm]
            wfree["o"] = [tm]

        f0 = {"ET": [], "E": [], "v": [], "eq": [], "A": [], "qs": {0: [], 1: []}, "ks": {0: [], 1: []}}
        za = put("dve", lambda e: e.memset(Ah[:].bitcast(F32), 0.0), sig="a_set")
        zb = put("dve", lambda e: e.memset(Al[:].bitcast(F32), 0.0), sig="a_set")
        put("dve", lambda e: e.memset(Ah[0:64, :, 128:129].bitcast(F32), 1.0), [za], sig="a_set")
        t_as = put("dve", lambda e: e.memset(Ah[64:128, :, 129:130].bitcast(F32), 1.0), [za], sig="a_set")
        r0 = {}

        def load_m0(b):
            im, mrow_, mw = mB.take()
            r0["m", b] = (im, mrow_, load("l_mB", mrow_[:], A["m0"][b].partition_broadcast(128), mw))

        def mask_m0(b):
            im, m, tm_ = r0["m", b]
            r0["m", b] = (im, m, put("dve", lambda e: e.tensor_scalar(m[:], m[:], 1.0, NEG, ALU.subtract, ALU.mult),
                                     [tm_], "mB"))

        def k0(b):
            p = b % 2
            im, mrow_, tmb = r0["m", b]
            for g in range(NC):
                i, bank, bw = work.take()
                for tm in product(bank, *channel_major("k", g), [state["w"]["k"], bw], "k_mm", xs["T"]):
                    yield 0.65
                j, kb, kw = vt.take()
                tk = put("dve", lambda e, k=kb, b_=bank, m=mrow_, g=g: e.tensor_tensor_reduce(
                    k[:], b_[:], m[:], 1.0, -3.0e38, ALU.add, ALU.max, kmx[:, p, g:g + 1]),
                    [tm, tmb, kw, f0["ks"][p]], "k_max")
                work.release(i, tk)
                t1 = put("dve", lambda e, g=g: e.tensor_tensor(kmb[:, p, g:g + 1], kmx[:, p, g:g + 1],
                                                               bkc[:, g:g + 1], ALU.add), [tk, state["bk_in"]], "k_mb")
                t1 = put("dve", lambda e, g=g: e.tensor_tensor(knb[:, p, g:g + 1], bkc[:, g:g + 1],
                                                               kmb[:, p, g:g + 1], ALU.subtract), [t1], "k_mb")
                te = put("act", lambda e, k=kb, g=g: e.activation(ET[:, g, :], k[:], ACT.Exp,
                                                                  bias=knb[:, p, g:g + 1],
                                                                  accum_out=ksm[:, p, g:g + 1]),
                         [tk, t1, f0["ET"], f0["ks"][p]], "k_exp")
                vt.release(j, te)
            mB.release(im, tk)
            if b + 1 < B:
                load_m0(b + 1)
            wfree["k"] = [tm]
            state["bk"] = [t1]
            r0["ET", b] = [te]
            r0["krc", b] = put("dve", lambda e: e.reciprocal(krc[:, p, :], ksm[:, p, :]), [te, f0["ks"][p]], "k_rc")

        def v0(b):
            for t in range(NT):
                i, bank, bw = work.take()
                for tm in product(bank, *token_major("v", t), [state["w"]["v"], bw], "v_mm", xs["T"]):
                    yield 0.65
                j, vb, vw = vt.take()
                ta = put("dve", lambda e, v=vb, b_=bank: e.tensor_tensor(v[:], b_[:], bvB[:], ALU.add),
                         [tm, state["bv_in"], vw], "v_add")
                work.release(i, ta)
                yield 0.1
                th = put("act", lambda e, v=vb, t=t: e.activation(vh[:, t, :], v[:], ACT.Identity,
                                                                  scale=mk[:, b, t:t + 1]), [ta, t_mk, f0["v"]], "v_hi")
                yield 0.2
                tl = put("dve", lambda e, v=vb, t=t: e.scalar_tensor_tensor(
                    out=vl[:, t, :], in0=v[:], scalar=mk[:, b, t:t + 1], in1=vh[:, t, :].bitcast(F32),
                    op0=ALU.mult, op1=ALU.subtract), [ta, th, f0["v"]], "v_lo")
                vt.release(j, th, tl)
            wfree["v"] = [tm]
            state["bv"] = [ta]
            r0["v", b] = [th, tl]

        def q0(b):
            for t in range(NT):
                i, bank, bw = work.take()
                for tm in product(bank, *token_major("q", t), [state["w"]["q"], bw], "q_mm", xs["T"]):
                    yield 0.65
                j, qb, qw = vt.take()
                ta = put("dve", lambda e, v=qb, b_=bank: e.tensor_tensor(v[:], b_[:], bqB[:], ALU.add),
                         [tm, state["bq_in"], qw], "q_add")
                work.release(i, ta)
                v3 = qb[:].rearrange("p (h d) -> p h d", h=H0)
                tx = put("dve", lambda e, v=v3, t=t: e.tensor_reduce(qmx[:, t % 2, :], v, AX.X, ALU.max),
                         [ta, f0["qs"][t % 2]], "q_max")
                tsb = put("pool", lambda e, v=v3, t=t: e.tensor_tensor(
                    v, v, qmx[:, t % 2, :].unsqueeze(2).to_broadcast([128, H0, 64]), ALU.subtract), [tx], "q_sub")
                f0["qs"][t % 2] = [tsb]
                yield 0.3
                te = put("act", lambda e, v=qb, t=t: e.activation(eq[:, t, :], v[:], ACT.Exp), [tsb, f0["eq"]], "q_exp")
                vt.release(j, te)
            wfree["q"] = [tm]
            state["bq"] = [ta]
            xs["free"] = [tm]
            r0["eq", b] = [te]

        def turn_e0(b):
            for t in range(NT):
                i, bank, bw = work.take()
                tt = turn(bank, [ET[:, g, t * 128:(t + 1) * 128] for g in range(NC)], [r0["ET", b], bw], "E_tr")
                th = put("act", lambda e, t=t, b_=bank: e.copy(Eh[:, t, :], b_[:]), [tt, f0["E"]], "E_hi")
                yield 0.3
                tl = put("dve", lambda e, t=t, b_=bank: e.tensor_tensor(
                    El[:, t, :], b_[:], Eh[:, t, :].bitcast(F32), ALU.subtract), [tt, th, f0["E"]], "E_lo")
                work.release(i, th, tl)
                yield 0.5
            if b + 1 < B:
                mask_m0(b + 1)
            f0["ET"] = [tt]
            r0["E", b] = [th, tl]

        def state0(b):
            p = b % 2
            i, bank, bw = work.take()
            for g in range(NC):
                def f(e, g=g, b_=bank):
                    n = slice(g * 128, (g + 1) * 128)
                    for t in range(NT):
                        e.matmul(b_[:, n], Eh[:, t, n], vh[:, t, n], start=(t == 0), stop=False)
                        e.matmul(b_[:, n], Eh[:, t, n], vl[:, t, n], start=False, stop=False)
                        r = e.matmul(b_[:, n], El[:, t, n], vh[:, t, n], start=False, stop=(t == NT - 1))
                    return r
                ta = put("pe", f, [r0["E", b], r0["v", b], bw], "att")
                yield 0.65
            f0["E"], f0["v"] = [ta], [ta]
            b3 = bank[:].rearrange("p (g n) -> p g n", g=NC)
            tz = []
            for h in range(2):
                r_ = slice(64 * h, 64 * h + 64)
                tf = put("dve", lambda e, r_=r_, h=h, b3=b3: e.tensor_tensor(
                    Af[r_], b3[r_, :, 64 * h:64 * h + 64],
                    krc[r_, p, :].unsqueeze(2).to_broadcast([64, NC, 64]), ALU.mult),
                    [ta, r0["krc", b], f0["A"]], "A_sc")
                tz.append(tf)
                th2 = put("act", lambda e, r_=r_, h=h: e.copy(Ah[r_, :, 64 * h:64 * h + 64], Af[r_]),
                          [tf, f0["A"], t_as], "A_hi")
                tl2 = put("dve", lambda e, r_=r_, h=h: e.tensor_tensor(
                    Al[r_, :, 64 * h:64 * h + 64], Af[r_], Ah[r_, :, 64 * h:64 * h + 64].bitcast(F32), ALU.subtract),
                    [tf, th2, f0["A"]], "A_lo")
            work.release(i, *tz)
            f0["ks"][p] = [tz[-1]]
            r0["A", b] = [th2, tl2]
            f0["Aw"] = [tl2]

        def y0(b):
            held = None
            for g in range(NC + 1):
                nxt = None
                if g < NC:
                    i, bank, bw = work.take()
                    tt = turn(bank, [eq[:, t, g * 128:(g + 1) * 128] for t in range(NT)], [r0["eq", b], bw], "q_tr")
                    jh, ah, wh_ = qh.take()
                    jl, al, wl_ = ql.take()
                    th = put("act", lambda e, a=ah, b_=bank: e.copy(a[:], b_[:]), [tt, wh_], "qT_hi")
                    yield 0.3
                    tl = put("dve", lambda e, a=al, h=ah, b_=bank: e.tensor_tensor(
                        a[:], b_[:], h[:].bitcast(F32), ALU.subtract), [tt, th, wl_], "qT_lo")
                    work.release(i, th, tl)
                    nxt = (g, jh, ah, jl, al, th, tl)
                    yield 0.5
                if held is not None:
                    hg, jh, ah, jl, al, th, tl = held
                    for half in range(2):
                        i, bank, bw = work.take()

                        def f(e, half=half, g=hg, b_=bank, ah=ah, al=al):
                            for u in range(2):
                                t = 2 * half + u
                                n, o = slice(t * 128, (t + 1) * 128), b_[:, u * 130:(u + 1) * 130]
                                e.matmul(o, ah[:, n], Ah[:, g, :], start=True, stop=False)
                                e.matmul(o, ah[:, n], Al[:, g, :], start=False, stop=False)
                                r = e.matmul(o, al[:, n], Ah[:, g, :], start=False, stop=True)
                            return r
                        tm = put("pe", f, [th, tl, r0["A", b], bw], "y_mm")
                        y3 = bank[:, 0:260].rearrange("p (u n) -> p u n", u=2)
                        tr = put("dve", lambda e, y3=y3: e.reciprocal(
                            yrc[:].rearrange("p (u h) -> p u h", u=2), y3[:, :, 128:130]),
                            [tm, f0.get("yrc", [])], "y_rc")
                        o4 = yb[:, 2 * half:2 * half + 2, hg * 128:(hg + 1) * 128]
                        ty = put("dve", lambda e, o4=o4, y3=y3: e.tensor_tensor(
                            o4.rearrange("p u (h d) -> p u h d", h=2),
                            y3[:, :, 0:128].rearrange("p u (h d) -> p u h d", h=2),
                            yrc[:].rearrange("p (u h) -> p u h", u=2).unsqueeze(3).to_broadcast([128, 2, 2, 64]),
                            ALU.mult), [tr, yfree["yb"]], "y_sc")
                        work.release(i, ty)
                        f0["yrc"] = [ty]
                        yield 0.45
                    qh.release(jh, tm)
                    ql.release(jl, tm)
                held = nxt
            f0["eq"] = [tt]
            f0["A"] = [tm]
            r0["y", b] = [ty] * NT

        s1 = {"stack": {0: [], 1: []}, "qsg": [], "ksg": [], "nx": {0: [], 1: []}, "rd": [], "nxd": [], "pv": [],
              "den": []}
        r1 = {}
        mf = {}

        def begin1(after):
            im, mt_, mw = vt.take()
            mrow, mrh, mrl = mt_[0:B, :], sg["q"][0:B, 0, :], sg["q"][0:B, 1, :]
            tm_ = load("l_mr", mrow, A["m1"], mw)
            t1 = put("dve", lambda e: e.tensor_scalar(mrow, mrow, 1.0, NEG, ALU.subtract, ALU.mult), [tm_], "mr")
            t2 = put("act", lambda e: e.copy(mrh, mrow), [t1, after], "mr_hi")
            t3 = put("dve", lambda e: e.tensor_tensor(mrl, mrow, mrh.bitcast(F32), ALU.subtract),
                     [t1, t2, after], "mr_lo")
            mf["m"] = [load("l_mrs0", md[0], mrh, [t2]), load("l_mrs1", md[1], mrl, [t3])]
            s1["qsg"] = mf["m"]
            vt.release(im, t2, t3)
            prev = t_sel
            for i in range(2):
                ta = put("pool", lambda e, i=i: e.memset(Qs[i][RM:RM + 32].bitcast(F32), 1.0), [after, prev], "st_set")
                tb_ = prev = put("pool", lambda e, i=i: e.memset(Ks[i][RM:RM + 32].bitcast(F32), 1.0),
                                 [after, ta], "st_set")
                s1["stack"][i] = [ta, tb_]
            state["set"] = [tb_]
            mf["after"] = after

        def v1(b, tiles=range(NT)):
            for t in tiles:
                i, bank, bw = work.take()
                for tm in product(bank, *token_major("v", t), [state["w"]["v"], bw], "v_mm", xs["T"]):
                    yield 0.65
                j, vb, vw = vt.take()
                ta = put("dve", lambda e, v=vb, b_=bank: e.tensor_tensor(v[:], b_[:], bvB[:], ALU.add),
                         [tm, state["bv_in"], vw], "v_add")
                work.release(i, ta)
                yield 0.2
                tv = put("act", lambda e, v=vb, t=t: e.activation(
                    xbuf(1, b)[:, t, :], v[:], ACT.Identity, scale=mk[:, b, t:t + 1]),
                    [ta, t_mk1, xs["turned", 1, b], mf["after"]], "v_out")
                vt.release(j, tv)
            wfree["v"] = [tm]
            r1["v", b] = [tv]

        def qk1(b, g):
            par = (4 * b + g) % 2
            for n in "qk":
                col = bqc if n == "q" else bkc
                i, bank, bw = work.take()
                for tm in product(bank, *channel_major(n, g), [state["w"][n], bw], n + "_mm", xs["T"]):
                    yield 0.65
                hi, lo = sg[n][:, 0, :], sg[n][:, 1, :]
                th = put("act", lambda e, a=hi, b_=bank, c=col: e.activation(
                    a, b_[:], ACT.Identity, bias=c[:, g:g + 1]),
                    [tm, s1[n + "sg"], mf["after"], state["b" + n + "_in"]], n + "_hi")
                yield 0.3
                tl = put("dve", lambda e, a=lo, h=hi, b_=bank, c=col: e.scalar_tensor_tensor(
                    out=a, in0=b_[:], scalar=c[:, g:g + 1], in1=h.bitcast(F32),
                    op0=ALU.add, op1=ALU.subtract), [tm, th, s1[n + "sg"], mf["after"]], n + "_lo")
                work.release(i, th, tl)
                ts = load(f"stq_{n}{par}", qkd[par, "qk".index(n)].rearrange("s p n -> p s n"), sg[n][:],
                          [th, tl, r1.get(("ld", n, par))])
                s1[n + "sg"] = [ts]
                r1[n, b, g] = ts
            if g == NG - 1:
                xs["free"] = [tm]

        def stack1(b, g):
            par = (4 * b + g) % 2
            free = [s1["stack"][par], mf["after"]]
            r1["stack", b, g] = []
            for n, S, rows in (("q", Qs[par], (0, 0, 1)), ("k", Ks[par], (0, 1, 0))):
                for r, p in enumerate(rows):
                    td = load(f"stk{n}{par}", S[32 * r:32 * r + 32, :, :],
                              qkd[par, "qk".index(n), p].rearrange("(j r) n -> r j n", r=32),
                              [r1[n, b, g], free])
                r1["ld", n, par] = [td]
                r1["stack", b, g].append(td)
            if g < 2:
                td = load(f"stm{par}", Ks[par][RM:RM + 2, :, :],
                          md[:, b, :].unsqueeze(1).to_broadcast([2, 4, T]), [mf["m"], free])
                r1["stack", b, g].append(td)

        def max1(b, g):
            par = (4 * b + g) % 2
            for j in range(4):
                for t in range(NT):
                    i, bank, bw = work.take()
                    tm = put("pe", lambda e, j=j, t=t, b_=bank: e.matmul(
                        b_[:], Qs[par][0:RX, j, t * 128:(t + 1) * 128], Ks[par][0:RX, j, :], start=True, stop=True),
                        [r1["stack", b, g], bw], "S")
                    tx = put("dve", lambda e, j=j, t=t, b_=bank: e.tensor_reduce(
                        nx[:, par, j * NT + t:j * NT + t + 1], b_[:], AX.X, ALU.max, negate=True),
                        [tm, s1["nx"][par], mf["after"]], "S_max")
                    work.release(i, tx)
                    yield 0.216
            yield 0.3
            i, bank, bw = work.take()
            tt = put("pe", lambda e, b_=bank: e.transpose(b_[0:16, 0:128], nx[:, par, :], ident[:]), [tx, bw], "nx_tr")
            th = put("act", lambda e, b_=bank: e.copy(nxh[:], b_[0:16, 0:128]), [tt, s1["nxd"]], "nx_hi")
            yield 0.1
            tl = put("dve", lambda e, b_=bank: e.tensor_tensor(
                nxl[:], b_[0:16, 0:128], nxh[:].bitcast(F32), ALU.subtract),
                [tt, th, s1["nxd"]], "nx_lo")
            work.release(i, th, tl)
            s1["nx"][par] = [tt]
            for r, src in ((RX, nxh), (RX + 1, nxl)):
                td = load(f"nxd{par}", Qs[par][r:r + 1, :, :].rearrange("p j (t n) -> p (j t) n", t=NT),
                          src[:], [th, tl, tm])
            s1["nxd"] = [td]
            r1["nx", b, g] = [td]

        def att1(b, g, after_st):
            par = (4 * b + g) % 2
            prev = None

            def pv(m, pb, te):
                def f(e, m=m, pb=pb):
                    for j in range(4):
                        h = 4 * g + j
                        r = e.matmul(PV[32 * j:32 * j + 32, :], xbuf(1, b)[:, m, h * 32:(h + 1) * 32], pb[:, j, :],
                                     start=(m == 0), stop=(m == NT - 1))
                    return r
                return put("pe", f, [te, r1["v", b], s1["pv"]], "PV")

            def add(j, m, acc, pb, pte, tk):
                eng = "dve" if (b, g) == (B - 1, NG - 1) and m > 1 else ADD[m - 1][j]
                return put(eng, lambda e: e.tensor_tensor(acc[:, j, :], acc[:, j, :], pb[:, j, :], ALU.add),
                           [pte[j], tk[j]], f"Ps_{eng}")

            tk = None
            for m in range(NT + 1):
                if m < NT:
                    ip, pb, pw = Pb.take()
                    te = []
                    for j in range(4):
                        i, bank, bw = work.take()
                        tm = put("pe", lambda e, j=j, m=m, b_=bank: e.matmul(
                            b_[:], Ks[par][0:RE, j, m * 128:(m + 1) * 128], Qs[par][0:RE, j, :], start=True, stop=True),
                            [r1["nx", b, g], bw], "ST")
                        te.append(put("act", lambda e, j=j, b_=bank, pb=pb: e.activation(
                            pb[:, j, :], b_[:], ACT.Exp), [tm, pw, mf["after"]], "P"))
                        work.release(i, te[-1])
                        yield 0.216
                        if m >= 2:
                            tk[j] = add(j, m - 1, pk, prev[2], prev[3], tk)
                    if m == NT - 1:
                        s1["stack"][par] = [tm]
                        if after_st is not None:
                            after_st()
                if prev is not None:
                    pm, pip, ppb, pte = prev
                    tpv = pv(pm, ppb, pte)
                    yield 1.1
                    if pm == 0:
                        ik, pk, tk = pip, ppb, [tpv] * 4
                    elif m < NT:
                        Pb.release(pip, tpv, *tk)
                if m < NT:
                    prev = (m, ip, pb, te)
            for j in range(4):
                tk[j] = add(j, NT - 1, pk, ppb, pte, tk)
            Pb.release(pip, tpv, *tk)
            iy, yT, yw = vt.take()
            tcy = put("act", lambda e: e.copy(yT[:], PV[:]), [tpv, yw], "yT")
            if g == NG - 1 and b + 2 < B:
                load_x(1, b + 2, [tpv, stored[0, b + 2]])
            r1["tail", b, g] = (iy, yT, tcy, tk, ik, pk)

        def tail1(b, g):
            iy, yT, tcy, tps, ik, pk = r1["tail", b, g]
            yield 0.2
            ta = turn(PV, [yT[:, t * 128:(t + 1) * 128] for t in range(NT)], [tcy], "y1_tr")
            vt.release(iy, ta)
            yield 0.1
            ty = put("act", lambda e: e.copy(yb[:, :, g * 128:(g + 1) * 128],
                                             PV[:].rearrange("p (t n) -> p t n", t=NT)), [ta, yfree["yb"]], "y1")
            s1["pv"] = [ty]
            yield 0.9

            def f(e):
                for j in range(4):
                    r = e.matmul(DEN[32 * j:32 * j + 32, :], sel[:, 4 - g:36 - g], pk[:, j, :],
                                 start=(g == 0), stop=(g == NG - 1))
                return r
            td = put("pe", f, [tps, s1["den"], t_sel], "den")
            Pb.release(ik, td)
            yield 1.1
            if g == NG - 1:
                idt, dT, dw = vt.take()
                tcd = put("act", lambda e: e.copy(dT[:], DEN[:]), [td, dw], "dT")
                yield 1.0
                tb_ = turn(DEN, [dT[:, t * 128:(t + 1) * 128] for t in range(NT)], [tcd], "d1_tr")
                vt.release(idt, tb_)
                tr = put("dve", lambda e: e.reciprocal(
                    rd[:].rearrange("p t g j -> p t j g"),
                    DEN[:].rearrange("p (t j l) -> p t j l", t=NT, j=4)[:, :, :, 0:4]),
                    [tb_, s1["rd"], mf["after"]], "rd")
                s1["den"] = [tr]
                ys_ = []
                for t in range(NT):
                    ys_.append(put("pool" if t % 2 else "dve", lambda e, t=t: e.tensor_tensor(
                        yb[:, t, :].rearrange("p (h l) -> p h l", h=H1),
                        yb[:, t, :].rearrange("p (h l) -> p h l", h=H1),
                        rd[:, t, :, :].rearrange("p g j -> p (g j)").unsqueeze(2).to_broadcast([128, H1, 32]),
                        ALU.mult), [ty, tr], f"y1_sc{t % 2}"))
                    yield 0.4
                s1["rd"] = ys_[-2:]
                yield from norm_y(1, b, ys_)

        def run(*gs):
            for _ in chain(*gs):
                pass

        spare = Ring([ET[:, c, :] for c in range(NC)], "x")

        def begin_w1():
            load_x(1, 0, [stored[0, 0], xs["turned", 0, B - 1]])
            spare.free = [(i, f0["ET"]) for i, _ in spare.free]
            prep_cols(1)
            return Stream(spare, load, [*w_items(1, "qkv")])

        load_x(0, 0, [])
        load_m0(0)
        prep_cols(0)
        w0 = Stream(wr, load, [*w_items(0, "kvqo"), *mod_items(0)])
        interleave((chain(prep_w(0, "k", w0), turn_x(0, 0)), 8.2, 0, 1), (norm_x(0, 0), 3.0, 0, 0.3))
        mask_m0(0)
        for b in range(B):
            past, first = b >= 1, b == 0
            interleave((k0(b), 10.4, 0, 1), (y0(b - 1) if past else None, 6.8, 0.05, 1),
                       (norm_x(0, b + 1) if b + 1 < B else None, 3.0, 0.3, 0.9),
                       (chain(prep_w(0, "v", w0), prep_w(0, "q", w0)) if first else None, 10.0, 0.2, 1))
            if first:
                prep_cols_end()
            interleave((v0(b), 11.6, 0, 1), (turn_e0(b), 3.2, 0.18, 0.85),
                       (norm_y(0, b - 1, r0["y", b - 1]) if past else None, 3.0, 0, 0.8),
                       (prep_w(0, "o", w0) if first else None, 4.0, 0, 1))
            interleave((q0(b), 11.6, 0, 1), (state0(b), 2.6, 0.35, 1),
                       (silu_y(0, b - 1) if past else None, 3.9, 0, 0.75),
                       (prep_mod(0, w0) if first else None, 16.2, 0, 1))
            if b + 1 == B:
                w1 = begin_w1()
            interleave((out_y(0, b - 1, range(NT)) if past else None, 10.4, 0.05, 1),
                       (turn_x(0, b + 1), 3.2, 0, 0.9) if b + 1 < B else
                       (chain(prep_w(1, "q", w1), prep_w(1, "k", w1)), 10.0, 0.25, 1),
                       (norm_x(1, 0) if b + 1 == B else None, 3.0, 0.4, 1))

        t_mk1 = load("l_mk1", mk[:], A["mk1"], [r0["v", B - 1]])
        interleave((prep_w(1, "v", w1), 5.0, 0, 0.9), (y0(B - 1), 6.8, 0, 1))
        prep_cols_end()
        after = list(flat([[w for _, w in spare.free], f0["A"], f0["E"], f0["v"], f0["eq"], f0["ET"], f0["yrc"], f0["ks"][0], f0["ks"][1],
                           r0["krc", B - 1], f0["Aw"], state["bq"], state["bk"]]))
        t_sel = put("pool", lambda e: e.memset(sel[:], 0.0), after, "sel")
        t_sel = put("pool", lambda e: e.memset(sel[:, 4:5], 1.0), [t_sel], "sel")
        begin1(after)
        load_x(1, 1, [stored[0, 1], after])
        interleave((chain(turn_x(1, 0), qk1(0, 0)), 9.0, 0, 1),
                   (chain(norm_y(0, B - 1, r0["y", B - 1]), silu_y(0, B - 1)), 6.2, 0, 1))
        stack1(0, 0)
        interleave((chain(v1(0), qk1(0, 1)), 15.6, 0, 1), (out_y(0, B - 1, range(NT)), 10.4, 0.2, 1))
        stack1(0, 1)
        s1["pv"], s1["den"] = [[w for i, w in work.free if ps[i] is bank] for bank in (PV, DEN)]
        work.free = [(i, w) for i, w in work.free if i < 6]

        w1 = Stream(wr, load, [*w_items(1, "o"), *mod_items(1)])
        run(max1(0, 0))
        seq = [(b, g) for b in range(B) for g in range(NG)]
        for n, (b, g) in enumerate(seq):
            nx1 = seq[n + 1] if n + 1 < len(seq) else None
            nx2 = seq[n + 2] if n + 2 < len(seq) else None
            fill, cost = [], 0.1
            if nx2:
                fill.append(qk1(*nx2))
                cost += 5.8
            if b == 0 and g < 3:
                fill += [prep_w(1, "o", w1) if g == 0 else prep_mod(1, w1, [g - 1])]
                cost += 4.0 if g == 0 else 8.1
            if g in (1, 2) and b >= 1:
                fill += [out_y(1, b - 1, range(2 * g - 2, 2 * g))]
                cost += 5.2
            if g == 1 and b + 1 < B:
                fill += [turn_x(1, b + 1)]
                cost += 3.2
            if g in (2, 3) and b + 1 < B:
                fill += [v1(b + 1, range(0, 1) if g == 2 else range(1, NT))]
                cost += 2.6 if g == 2 else 7.8
            interleave((att1(b, g, (lambda: stack1(*nx2)) if nx2 else None), 7.8, 0.03, 1),
                       (tail1(*seq[n - 1]) if n else None, 2.3 if seq[n - 1][1] < NG - 1 else 7.9, 0, 0.3 if seq[n - 1][1] < NG - 1 else 0.5),
                       (norm_x(1, b + 1) if g == 1 and b + 1 < B else None, 3.0, 0.05, 0.4),
                       (silu_y(1, b - 1) if g == 0 and b >= 1 else None, 3.8, 0.55, 1),
                       (max1(*nx1) if nx1 else None, 3.9, 0.03, 0.78),
                       (chain(*fill) if fill else None, cost, 0, min(1, 0.68 * cost / 5.8)))
        run(tail1(B - 1, NG - 1), silu_y(1, B - 1), out_y(1, B - 1, range(NT)))
        for j in range(4):
            c = Q.sem(f"st{j}")
            Q.q["sp"].append((lambda e: None, [(c, c.n)], None, 16))
        block = ctx.enter_context(nc.Block())

        @block.sync
        def _(e):
            Q.run("sp", e)

        @block.gpsimd
        def _(e):
            Q.run("pool", e)

        @block.scalar
        def _(e):
            Q.run("act", e)

        @block.vector
        def _(e):
            Q.run("dve", e)

        @block.tensor
        def _(e):
            Q.run("pe", e)


def kernel(**inputs):
    import numpy as np
    import concourse.bacc as bacc
    from concourse import mybir as mb
    from concourse.bass_utils import run_bass_kernel_spmd

    g = {k: np.asarray(v) for k, v in inputs.items()}

    def col(v):
        return v.reshape(NC, 128).T

    def mcol(m):
        return np.ascontiguousarray(m.reshape(B, NT, 128).transpose(2, 0, 1))

    P0, P1 = "L0_cond_", "L1_cond_"
    a = {
        "x": g["x"],
        "m0": g["mask_BxSx1_fk1"].reshape(B, T),
        "m1": g["mask_BxS_ff1"],
        "mk": mcol(g["mask_BxSx1_fk1"]),
        "mk1": mcol(g["mask_BxS_ff1"]),
        "cT": np.ascontiguousarray(g["cond_2048"].T.reshape(8, 128, B).transpose(1, 0, 2)),
        "cols0": np.concatenate([col(g[P0 + n]) for n in ("ln_w", "ln_b", "ln2_w", "ln2_b")], axis=1),
        "cols1": np.concatenate([col(g[P1 + n]) for n in ("norm_w", "norm_b", "sb_norm_w", "sb_norm_b")], axis=1),
        "Wq0": g[P0 + "Wq"], "bq0": g[P0 + "bq"], "Wk0": g[P0 + "Wk"], "bk0": g[P0 + "bk"],
        "Wv0": g[P0 + "Wv"], "bv0": g[P0 + "bv"], "We0": g[P0 + "W_emb"], "be0": g[P0 + "b_emb"],
        "Wo0": g[P0 + "W_out"], "bo0": g[P0 + "b_out"],
        "Wq1": g[P1 + "q_w"], "bq1": g[P1 + "q_b"], "Wk1": g[P1 + "k_w"], "bk1": g[P1 + "k_b"],
        "Wv1": g[P1 + "v_w"], "bv1": g[P1 + "v_b"], "We1": g[P1 + "emb_w"], "be1": g[P1 + "emb_b"],
        "Wo1": g[P1 + "out_w"], "bo1": g[P1 + "out_b"],
    }
    nc = bacc.Bacc("TRN2", target_bir_lowering=False, num_devices=1)
    arrays, aps = {}, {}
    for n, v in a.items():
        v = np.ascontiguousarray(v)
        arrays["in_" + n] = v
        aps[n] = nc.dram_tensor("in_" + n, v.shape, mb.dt.from_np(v.dtype), kind="ExternalInput").ap()
    out = nc.dram_tensor("out_0", (B, T, D), mb.dt.float32, kind="ExternalOutput").ap()
    cond_two_layers(nc, aps, out)
    r = run_bass_kernel_spmd(nc, [arrays], core_ids=[0])
    return r.results[0]["out_0"]
```
